# Optimizing a Trainium2 kernel written in Bass

```python
import numpy as np
import jax
import jax.numpy as jnp

def _softmax(x, axis=-1):
    return jax.nn.softmax(x, axis=axis)

def _gelu(x):
    return jax.nn.gelu(x, approximate=True)

def _silu(x):
    return jax.nn.silu(x)

def _sigmoid(x):
    return jax.nn.sigmoid(x)

def _layernorm(x, axis=-1, eps=1e-05):
    m = jnp.mean(x, axis=axis, keepdims=True)
    v = jnp.var(x, axis=axis, keepdims=True)
    return (x - m) / jnp.sqrt(v + eps)

def _scatter_add(tgt, idx, src, axis=0):
    return tgt.at[idx].add(src)

def _segment_sum(src, seg, n):
    return jax.ops.segment_sum(src, seg, n)
kernel_name = 'mk_gnn_resnorm_d4_gnn_r8_401224'

def setup_inputs(seed: int=0):
    np.random.seed(seed)
    _w = jnp.asarray

    def _rec_inputs():
        import jax
        import jax.numpy as jnp
        _gk = jax.random.key(seed)
        x = -0.000202 + 1 * jax.random.normal(jax.random.fold_in(_gk, 1), (6250, 128), jnp.float32)
        src = jax.random.randint(jax.random.fold_in(_gk, 2), (100000,), 0, 6250, jnp.int32)
        dst = jax.random.randint(jax.random.fold_in(_gk, 3), (100000,), 0, 6250, jnp.int32)
        _o = jnp.argsort(dst, stable=True)
        src = src[_o]
        dst = dst[_o]
        edge_attr_32 = 0.000268479 + 0.999861 * jax.random.normal(jax.random.fold_in(_gk, 12), (100000, 32), jnp.float32)
        edge_weight = jax.random.uniform(jax.random.fold_in(_gk, 14), (100000,), jnp.float32, 0.0, 1)
        return (x, src, dst, edge_attr_32, edge_weight)
    x, src, dst, edge_attr_32, edge_weight = _rec_inputs()

    def _L0_gnn_setup():
        import jax, jax.numpy as jnp
        import numpy as np
        N_NODES = 6250
        N_EDGES = 100000
        IN_FEAT = 128
        OUT_FEAT = 128
        key = jax.random.key(seed)
        ks = jax.random.split(key, 9)
        s = 1.0 / np.sqrt(IN_FEAT)
        return {'x': jax.random.normal(ks[0], (N_NODES, IN_FEAT), dtype=jnp.float32), 'src': jax.random.randint(ks[1], (N_EDGES,), 0, N_NODES), 'dst': jax.random.randint(ks[2], (N_EDGES,), 0, N_NODES), 'W1': jax.random.uniform(ks[3], (IN_FEAT, OUT_FEAT), jnp.float32, -s, s), 'b1': jax.random.uniform(ks[4], (OUT_FEAT,), jnp.float32, -s, s), 'W2': jax.random.uniform(ks[5], (OUT_FEAT, 1), jnp.float32, -s, s), 'b2': jax.random.uniform(ks[6], (1,), jnp.float32, -s, s), 'W4': jax.random.uniform(ks[7], (IN_FEAT, OUT_FEAT), jnp.float32, -s, s), 'b4': jax.random.uniform(ks[8], (OUT_FEAT,), jnp.float32, -s, s)}
    _L0_gnn_all = _L0_gnn_setup()
    _L0_gnn_in = {k: v for k, v in _L0_gnn_all.items() if k in ('W1', 'b1', 'W2', 'b2', 'W4', 'b4')}
    del _L0_gnn_all

    def _L1_gnn_setup():
        import jax, jax.numpy as jnp
        import numpy as np
        N = 12500
        E = 200000
        DIN = 128
        DOUT = 128
        H = 4
        DS = DOUT // H

        def _lrelu(x):
            return jnp.where(x > 0, x, 0.2 * x)
        key = jax.random.key(seed)
        ks = jax.random.split(key, 8)
        feat_in = jax.random.normal(ks[0], (N, DIN), dtype=jnp.float32)
        edge_row = jnp.sort(jax.random.randint(ks[1], (E,), 0, N, dtype=jnp.int32))
        edge_col = jax.random.randint(ks[2], (E,), 0, N, dtype=jnp.int32)
        edge_val = jnp.ones((E,), dtype=jnp.float32)
        lim = 1.0 / np.sqrt(DIN)
        W0 = jax.random.uniform(ks[3], (DOUT, DIN), minval=-lim, maxval=lim, dtype=jnp.float32)
        b0 = jnp.zeros((DOUT,), dtype=jnp.float32)
        W1 = jax.random.uniform(ks[4], (DOUT, DIN), minval=-lim, maxval=lim, dtype=jnp.float32)
        b1 = jnp.zeros((DOUT,), dtype=jnp.float32)
        glim = np.sqrt(6.0 / (2 * H * DS))
        attention = jax.random.uniform(ks[5], (2, H, DS), minval=-glim, maxval=glim, dtype=jnp.float32)
        scale = jnp.ones((2, H, DS), dtype=jnp.float32)
        offset = jnp.zeros((2, H, DS), dtype=jnp.float32)
        return {'feat_in': feat_in, 'edge_row': edge_row, 'edge_col': edge_col, 'edge_val': edge_val, 'W0': W0, 'b0': b0, 'W1': W1, 'b1': b1, 'attention': attention, 'scale': scale, 'offset': offset}
    _L1_gnn_all = _L1_gnn_setup()
    _L1_gnn_in = {k: v for k, v in _L1_gnn_all.items() if k in ('W0', 'b0', 'W1', 'b1', 'attention', 'scale', 'offset')}
    del _L1_gnn_all

    def _L2_gnn_setup():
        import jax, jax.numpy as jnp
        import numpy as np
        N, E = (1250, 40000)
        H, NH, ED = (128, 8, 32)
        HD = H // NH
        FF = 4 * H

        def _layer_norm(x, g, b, eps=1e-05):
            m = jnp.mean(x, axis=-1, keepdims=True)
            v = jnp.mean((x - m) ** 2, axis=-1, keepdims=True)
            return (x - m) / jnp.sqrt(v + eps) * g + b
        key = jax.random.key(seed)
        ks = jax.random.split(key, 16)

        def p(k, shape, fan_in):
            return jax.random.normal(k, shape, jnp.float32) * fan_in ** (-0.5)
        return {'x': jax.random.normal(ks[0], (N, H), jnp.float32), 'edge_index': jax.random.randint(ks[1], (2, E), 0, N, dtype=jnp.int32).astype(jnp.int64), 'edge_attr': jax.random.normal(ks[2], (E, ED), jnp.float32), 'Wq': p(ks[3], (H, H), H), 'bq': jnp.zeros((H,), jnp.float32), 'Wk': p(ks[4], (H, H), H), 'bk': jnp.zeros((H,), jnp.float32), 'Wv': p(ks[5], (H, H), H), 'bv': jnp.zeros((H,), jnp.float32), 'We': p(ks[6], (ED, NH), ED), 'be': jnp.zeros((NH,), jnp.float32), 'Wo': p(ks[7], (H, H), H), 'bo': jnp.zeros((H,), jnp.float32), 'ln1_g': jnp.ones((H,), jnp.float32), 'ln1_b': jnp.zeros((H,), jnp.float32), 'W1': p(ks[8], (H, FF), H), 'b1': jnp.zeros((FF,), jnp.float32), 'W2': p(ks[9], (FF, H), FF), 'b2': jnp.zeros((H,), jnp.float32), 'ln2_g': jnp.ones((H,), jnp.float32), 'ln2_b': jnp.zeros((H,), jnp.float32)}
    _L2_gnn_all = _L2_gnn_setup()
    _L2_gnn_in = {k: v for k, v in _L2_gnn_all.items() if k in ('Wq', 'bq', 'Wk', 'bk', 'Wv', 'bv', 'We', 'be', 'Wo', 'bo', 'ln1_g', 'ln1_b', 'W1', 'b1', 'W2', 'b2', 'ln2_g', 'ln2_b')}
    del _L2_gnn_all

    def _L3_gnn_setup():
        import jax, jax.numpy as jnp
        import numpy as np
        NEG_SLOPE = 0.2

        def _gat_layer(x, src, dst, W, a_s, a_d, b, num_nodes):
            H, C = a_s.shape
            h = (x @ W).reshape(num_nodes, H, C)
            alpha_src = jnp.einsum('nhc,hc->nh', h, a_s)
            alpha_dst = jnp.einsum('nhc,hc->nh', h, a_d)
            e = jax.nn.leaky_relu(alpha_src[src] + alpha_dst[dst], NEG_SLOPE)
            m = jax.lax.stop_gradient(jax.ops.segment_max(e, dst, num_segments=num_nodes))
            e = jnp.exp(e - m[dst])
            den = jax.ops.segment_sum(e, dst, num_segments=num_nodes)
            alpha = e / den[dst]
            msg = h[src] * alpha[:, :, None]
            out = jax.ops.segment_sum(msg, dst, num_segments=num_nodes)
            return out.reshape(num_nodes, H * C) + b
        key = jax.random.key(seed)
        ks = jax.random.split(key, 10)
        N, E, D, H, C = (12500, 200000, 128, 4, 32)
        s = 1.0 / np.sqrt(D)
        return {'x': jax.random.normal(ks[0], (N, D), jnp.float32), 'edge_index': jax.random.randint(ks[1], (2, E), 0, N, jnp.int64), 'W1': jax.random.normal(ks[2], (D, H * C), jnp.float32) * s, 'a_src1': jax.random.normal(ks[3], (H, C), jnp.float32) * s, 'a_dst1': jax.random.normal(ks[4], (H, C), jnp.float32) * s, 'b1': jnp.zeros((H * C,), jnp.float32), 'W2': jax.random.normal(ks[5], (H * C, H * C), jnp.float32) * s, 'a_src2': jax.random.normal(ks[6], (H, C), jnp.float32) * s, 'a_dst2': jax.random.normal(ks[7], (H, C), jnp.float32) * s, 'b2': jnp.zeros((H * C,), jnp.float32)}
    _L3_gnn_all = _L3_gnn_setup()
    _L3_gnn_in = {k: v for k, v in _L3_gnn_all.items() if k in ('W1', 'a_src1', 'a_dst1', 'b1', 'W2', 'a_src2', 'a_dst2', 'b2')}
    del _L3_gnn_all
    return {'x': x, 'src': src, 'dst': dst, 'edge_attr_32': edge_attr_32, 'edge_weight': edge_weight, 'L0_gnn_W1': _L0_gnn_in['W1'], 'L0_gnn_b1': _L0_gnn_in['b1'], 'L0_gnn_W2': _L0_gnn_in['W2'], 'L0_gnn_b2': _L0_gnn_in['b2'], 'L0_gnn_W4': _L0_gnn_in['W4'], 'L0_gnn_b4': _L0_gnn_in['b4'], 'L1_gnn_W0': _L1_gnn_in['W0'], 'L1_gnn_b0': _L1_gnn_in['b0'], 'L1_gnn_W1': _L1_gnn_in['W1'], 'L1_gnn_b1': _L1_gnn_in['b1'], 'L1_gnn_attention': _L1_gnn_in['attention'], 'L1_gnn_scale': _L1_gnn_in['scale'], 'L1_gnn_offset': _L1_gnn_in['offset'], 'L2_gnn_Wq': _L2_gnn_in['Wq'], 'L2_gnn_bq': _L2_gnn_in['bq'], 'L2_gnn_Wk': _L2_gnn_in['Wk'], 'L2_gnn_bk': _L2_gnn_in['bk'], 'L2_gnn_Wv': _L2_gnn_in['Wv'], 'L2_gnn_bv': _L2_gnn_in['bv'], 'L2_gnn_We': _L2_gnn_in['We'], 'L2_gnn_be': _L2_gnn_in['be'], 'L2_gnn_Wo': _L2_gnn_in['Wo'], 'L2_gnn_bo': _L2_gnn_in['bo'], 'L2_gnn_ln1_g': _L2_gnn_in['ln1_g'], 'L2_gnn_ln1_b': _L2_gnn_in['ln1_b'], 'L2_gnn_W1': _L2_gnn_in['W1'], 'L2_gnn_b1': _L2_gnn_in['b1'], 'L2_gnn_W2': _L2_gnn_in['W2'], 'L2_gnn_b2': _L2_gnn_in['b2'], 'L2_gnn_ln2_g': _L2_gnn_in['ln2_g'], 'L2_gnn_ln2_b': _L2_gnn_in['ln2_b'], 'L3_gnn_W1': _L3_gnn_in['W1'], 'L3_gnn_a_src1': _L3_gnn_in['a_src1'], 'L3_gnn_a_dst1': _L3_gnn_in['a_dst1'], 'L3_gnn_b1': _L3_gnn_in['b1'], 'L3_gnn_W2': _L3_gnn_in['W2'], 'L3_gnn_a_src2': _L3_gnn_in['a_src2'], 'L3_gnn_a_dst2': _L3_gnn_in['a_dst2'], 'L3_gnn_b2': _L3_gnn_in['b2']}

def reference(x, src, dst, edge_attr_32, edge_weight, L0_gnn_W1, L0_gnn_b1, L0_gnn_W2, L0_gnn_b2, L0_gnn_W4, L0_gnn_b4, L1_gnn_W0, L1_gnn_b0, L1_gnn_W1, L1_gnn_b1, L1_gnn_attention, L1_gnn_scale, L1_gnn_offset, L2_gnn_Wq, L2_gnn_bq, L2_gnn_Wk, L2_gnn_bk, L2_gnn_Wv, L2_gnn_bv, L2_gnn_We, L2_gnn_be, L2_gnn_Wo, L2_gnn_bo, L2_gnn_ln1_g, L2_gnn_ln1_b, L2_gnn_W1, L2_gnn_b1, L2_gnn_W2, L2_gnn_b2, L2_gnn_ln2_g, L2_gnn_ln2_b, L3_gnn_W1, L3_gnn_a_src1, L3_gnn_a_dst1, L3_gnn_b1, L3_gnn_W2, L3_gnn_a_src2, L3_gnn_a_dst2, L3_gnn_b2):
    import jax
    import jax.numpy as jnp

    def _L0_gnn_ref(x, src, dst, W1, b1, W2, b2, W4, b4):
        import jax, jax.numpy as jnp
        import numpy as np
        N_NODES = 6250
        N_EDGES = 100000
        IN_FEAT = 128
        OUT_FEAT = 128
        n_nodes = x.shape[0]
        theta = x[dst] - x[src]
        w = jax.nn.sigmoid(jax.nn.relu(theta @ W1 + b1) @ W2 + b2)
        w_theta = w * theta
        agg = jax.ops.segment_sum(w_theta, dst, num_segments=n_nodes)
        indeg = jax.ops.segment_sum(jnp.ones((dst.shape[0], 1), x.dtype), dst, num_segments=n_nodes)
        return agg + indeg * (x @ W4 + b4)

    def _L1_gnn_ref(feat_in, edge_row, edge_col, edge_val, W0, b0, W1, b1, attention, scale, offset):
        import jax, jax.numpy as jnp
        import numpy as np
        N = 12500
        E = 200000
        DIN = 128
        DOUT = 128
        H = 4
        DS = DOUT // H

        def _lrelu(x):
            return jnp.where(x > 0, x, 0.2 * x)
        n = feat_in.shape[0]
        h_self = jax.nn.relu(feat_in @ W0.T + b0).reshape(n, H, DS)
        h_neigh = jax.nn.relu(feat_in @ W1.T + b1).reshape(n, H, DS)
        att_self = _lrelu(jnp.einsum('nhd,hd->nh', h_self, attention[0]))
        att_neigh = _lrelu(jnp.einsum('nhd,hd->nh', h_neigh, attention[1]))
        val = att_self[edge_row] + att_neigh[edge_col]
        mx = jax.ops.segment_max(val, edge_row, num_segments=n)
        val_exp = jnp.exp(val - mx[edge_row]) * edge_val[:, None]
        denom = jnp.clip(jax.ops.segment_sum(val_exp, edge_row, num_segments=n), 1e-10)
        msg = val_exp[:, :, None] * h_neigh[edge_col]
        agg = jax.ops.segment_sum(msg, edge_row, num_segments=n) / denom[:, :, None]

        def norm_feat(x, b):
            mean = x.mean(axis=-1, keepdims=True)
            var = x.var(axis=-1, keepdims=True) + 1e-09
            return (x - mean) * scale[b] * jax.lax.rsqrt(var) + offset[b]
        feat_neigh = norm_feat(agg, 0)
        feat_self = norm_feat(h_self, 1)
        return ((feat_self + feat_neigh) * 0.5).reshape(n, H * DS)

    def _L2_gnn_ref(x, edge_index, edge_attr, Wq, bq, Wk, bk, Wv, bv, We, be, Wo, bo, ln1_g, ln1_b, W1, b1, W2, b2, ln2_g, ln2_b):
        import jax, jax.numpy as jnp
        import numpy as np
        N, E = (1250, 40000)
        H, NH, ED = (128, 8, 32)
        HD = H // NH
        FF = 4 * H

        def _layer_norm(x, g, b, eps=1e-05):
            m = jnp.mean(x, axis=-1, keepdims=True)
            v = jnp.mean((x - m) ** 2, axis=-1, keepdims=True)
            return (x - m) / jnp.sqrt(v + eps) * g + b
        n = x.shape[0]
        src, dst = (edge_index[0], edge_index[1])
        q = (x @ Wq + bq).reshape(n, NH, HD)
        k = (x @ Wk + bk).reshape(n, NH, HD)
        v = (x @ Wv + bv).reshape(n, NH, HD)
        edge_bias = edge_attr @ We + be
        scores = jnp.sum(q[src] * k[dst], axis=-1) / jnp.sqrt(jnp.float32(HD)) + edge_bias
        mx = jax.ops.segment_max(scores, dst, num_segments=n)
        ex = jnp.exp(scores - mx[dst])
        den = jax.ops.segment_sum(ex, dst, num_segments=n)
        attn = ex / (den[dst] + 1e-08)
        agg = jax.ops.segment_sum(v[src] * attn[..., None], dst, num_segments=n)
        out = agg.reshape(n, H) @ Wo + bo
        x = _layer_norm(x + out, ln1_g, ln1_b)
        h = jax.nn.gelu(x @ W1 + b1, approximate=False) @ W2 + b2
        return _layer_norm(x + h, ln2_g, ln2_b)

    def _L3_gnn_ref(x, edge_index, W1, a_src1, a_dst1, b1, W2, a_src2, a_dst2, b2):
        import jax, jax.numpy as jnp
        import numpy as np
        NEG_SLOPE = 0.2

        def _gat_layer(x, src, dst, W, a_s, a_d, b, num_nodes):
            H, C = a_s.shape
            h = (x @ W).reshape(num_nodes, H, C)
            alpha_src = jnp.einsum('nhc,hc->nh', h, a_s)
            alpha_dst = jnp.einsum('nhc,hc->nh', h, a_d)
            e = jax.nn.leaky_relu(alpha_src[src] + alpha_dst[dst], NEG_SLOPE)
            m = jax.lax.stop_gradient(jax.ops.segment_max(e, dst, num_segments=num_nodes))
            e = jnp.exp(e - m[dst])
            den = jax.ops.segment_sum(e, dst, num_segments=num_nodes)
            alpha = e / den[dst]
            msg = h[src] * alpha[:, :, None]
            out = jax.ops.segment_sum(msg, dst, num_segments=num_nodes)
            return out.reshape(num_nodes, H * C) + b
        N = x.shape[0]
        loop = jnp.arange(N, dtype=edge_index.dtype)
        src = jnp.concatenate([edge_index[0], loop])
        dst = jnp.concatenate([edge_index[1], loop])
        h = _gat_layer(x, src, dst, W1, a_src1, a_dst1, b1, N)
        h = jax.nn.relu(h)
        h = _gat_layer(h, src, dst, W2, a_src2, a_dst2, b2, N)
        return jax.nn.relu(h)
    edge_index = jnp.stack([src, dst])
    x = _layernorm(x + _L0_gnn_ref(x, src, dst, L0_gnn_W1, L0_gnn_b1, L0_gnn_W2, L0_gnn_b2, L0_gnn_W4, L0_gnn_b4), axis=-1)
    x = _layernorm(x + _L1_gnn_ref(x, src, dst, edge_weight, L1_gnn_W0, L1_gnn_b0, L1_gnn_W1, L1_gnn_b1, L1_gnn_attention, L1_gnn_scale, L1_gnn_offset), axis=-1)
    x = _layernorm(x + _L2_gnn_ref(x, edge_index, edge_attr_32, L2_gnn_Wq, L2_gnn_bq, L2_gnn_Wk, L2_gnn_bk, L2_gnn_Wv, L2_gnn_bv, L2_gnn_We, L2_gnn_be, L2_gnn_Wo, L2_gnn_bo, L2_gnn_ln1_g, L2_gnn_ln1_b, L2_gnn_W1, L2_gnn_b1, L2_gnn_W2, L2_gnn_b2, L2_gnn_ln2_g, L2_gnn_ln2_b), axis=-1)
    x = _layernorm(x + _L3_gnn_ref(x, edge_index, L3_gnn_W1, L3_gnn_a_src1, L3_gnn_a_dst1, L3_gnn_b1, L3_gnn_W2, L3_gnn_a_src2, L3_gnn_a_dst2, L3_gnn_b2), axis=-1)
    return x

_drawn_inputs = setup_inputs


def setup_inputs(seed=0):
    import zlib

    import numpy as np

    out = dict(_drawn_inputs(seed))
    spreads = {'L1_gnn_b0': (0.0, 0.1),
     'L1_gnn_b1': (0.0, 0.1),
     'L1_gnn_scale': (1.0, 0.2),
     'L1_gnn_offset': (0.0, 0.1),
     'L2_gnn_bq': (0.0, 2.0),
     'L2_gnn_bk': (0.0, 0.495),
     'L2_gnn_bv': (0.0, 0.1),
     'L2_gnn_be': (0.0, 2.0),
     'L2_gnn_bo': (0.0, 0.1),
     'L2_gnn_ln1_g': (1.0, 0.2),
     'L2_gnn_ln1_b': (0.0, 0.1),
     'L2_gnn_b1': (0.0, 0.294),
     'L2_gnn_b2': (0.0, 0.1),
     'L2_gnn_ln2_g': (1.0, 0.2),
     'L2_gnn_ln2_b': (0.0, 0.1),
     'L3_gnn_b1': (0.0, 0.1),
     'L3_gnn_b2': (0.0, 0.1)}
    factors = {'L0_gnn_b1': 24.602,
     'L3_gnn_a_dst1': 54.229,
     'L3_gnn_a_src2': 30.56,
     'L3_gnn_a_dst2': 55.379}
    for name, (base, spread) in spreads.items():
        noise = np.random.default_rng([zlib.crc32(name.encode()), seed]).standard_normal(out[name].shape)
        drawn = base * np.exp(spread * noise) if base else spread * noise
        out[name] = jnp.asarray(drawn.astype(out[name].dtype))
    for name, factor in factors.items():
        out[name] = (out[name] * factor).astype(out[name].dtype)
    return out
```

```python
import concourse.bass as bass
from concourse import mybir
from contextlib import ExitStack

F32 = mybir.dt.float32
I32 = mybir.dt.int32
BF16 = mybir.dt.bfloat16
ALU = mybir.AluOpType
ACT = mybir.ActivationFunctionType
AX = mybir.AxisListType

N = 6250
E = 100000
D = 128
P = 128
CH = 784
EP = P * CH
B = 14
NG = CH // B
IT = NG // 2
NB = 49
NP = NB * P
KB = 7
KG = NB // KB
LASTV = E - (P - 1) * CH
ROWS = N - (NB - 1) * P
BIG = 1e30
BQ = EP // P

HEADS = [1, 4, 8, 4, 4]
HD1 = [129, 33, 17, 33, 33]
FW = [h * d for h, d in zip(HEADS, HD1)]
GW = [257, 136, 264, 136, 136]
VO = [128, 0, 128, 0, 0]
SW = [129, 136, 144, 136, 136]
ZW = [128, 0, 128, 4, 4]
GMAX, SMAX = max(GW), max(SW)

BIAS = ["L0_gnn_b1", "L0_gnn_W2", "L0_gnn_b4", "L1_gnn_b0", "L1_gnn_b1", "att", "scale0", "scale1",
        "offset0", "offset1", "L2_gnn_bq", "L2_gnn_bk", "L2_gnn_bv", "L2_gnn_bo", "L2_gnn_ln1_g",
        "L2_gnn_ln1_b", "L2_gnn_b2", "L2_gnn_ln2_g", "L2_gnn_ln2_b", "L3_gnn_b1", "L3_gnn_b2",
        "L3_gnn_a_src1", "L3_gnn_a_dst1", "L3_gnn_a_src2", "L3_gnn_a_dst2"]


class Steps:

    def __init__(self, sem, start=0):
        self.sem, self.base, self.k, self.it, self.per = sem, start, 0, None, 0

    def loop(self, it, per):
        self.it, self.per, self.k = it, per, 0

    def close(self, turns):
        assert self.k == self.per, (str(self.sem), self.k, self.per)
        self.base += turns * self.per
        self.it, self.k = None, 0

    def add(self, by=1):
        if self.it is None:
            self.base += by
        else:
            self.k += by

    def value(self):
        return self.base if self.it is None else self.it * self.per + (self.base + self.k)


def build(nc, a, out):
    with ExitStack() as ctx:
        def sb(name, shape, dt=F32):
            return ctx.enter_context(nc.sbuf_tensor(name, shape, dt))

        def sem(name):
            return ctx.enter_context(nc.semaphore(name))

        def dram(name, shape, dt=F32):
            return nc.dram_tensor(name, shape, dt, kind="Internal").ap()

        table = [dram(f"table{p}", [NP, GW[p]]) for p in range(5)]
        dst_table = {p: dram(f"dst_table{p}", [NP, ZW[p]]) for p in (0, 2, 3, 4)}
        spread_wide = dram("spread_wide", [EP, D])
        spread_slim = dram("spread_slim", [EP, 4])
        spread = {0: spread_wide, 2: spread_wide, 3: spread_slim, 4: spread_slim}
        states_by_width = {w: dram(f"states{w}", [EP + 1, w]) for w in sorted(set(SW))}
        states = [states_by_width[w] for w in SW]
        attr_pad = dram("attr_pad", [EP, 32])
        dst_rows = dram("dst_rows", [BQ, P])
        samples = dram("samples", [BQ])
        ends = dram("ends", [NP + 1, 1])
        ends_src = dram("ends_src", [NP, 1])
        low_rows = dram("low_rows", [CH, P])
        by_src = dram("by_src", [EP, 3])

        rows = sb("rows", [P, 2 * B * GMAX])
        dstf = sb("dstf", [P, 2, B, D])
        sums = sb("sums", [P, 2 * B * SMAX])
        msg = sb("msg", [P, B * max(FW)])
        ebuf = sb("ebuf", [P, 8 * CH])
        X = sb("X", [P, NB, D])
        aux = sb("aux", [P, NB, 136])
        src = sb("src", [P, CH + 2 * B], I32)
        cont = sb("cont", [P, CH])
        src1 = sb("src1", [P, CH + 2 * B], I32)
        cont1 = sb("cont1", [P, CH])
        colf = sb("colf", [P, P])
        payload = sb("payload", [P, 2, B, 3])
        place = sb("place", [P, 2, B], I32)
        lowg = sb("lowg", [P, B])
        spot = sb("spot", [P, B])
        ew = sb("ew", [P, CH])
        bias = sb("bias", [P, len(BIAS), D])
        ident = sb("ident", [P, P])
        ones = sb("ones", [P, P])
        chains = [sb(f"chain{k}", [P, P]) for k in range(2)]
        fars = [sb(f"far{k}", [P, P]) for k in range(2)]
        WA = [sb(f"WA{p}", [P, 256 if p < 3 else 136]) for p in range(5)]
        Wv = sb("Wv", [P, D])
        Wo = sb("Wo", [P, D])
        W1 = sb("W1", [P, 4 * D])
        W2 = sb("W2", [P, 4, D])
        Web = sb("Web", [P, 32])
        beb = sb("beb", [P, 8])
        b2b = sb("b2b", [P, 1])
        b1c = sb("b1c", [P, 4])
        eps = sb("eps", [P, 2])
        attr = sb("attr", [P, 2, B * 32])
        attrT = sb("attrT", [P, 512])
        idx = sb("idx", [P, 2, B], I32)
        cg = sb("cg", [P, 2, B])
        nf = sb("nf", [P, 8 * (B + 1) + 1])
        sc = sb("sc", [P, 8 * (B + 1)])
        fm = sb("fm", [P, 8 * (B + 1)])
        mx = sb("mx", [P, 8 * (B + 1)])
        df = sb("df", [P, 8 * (B + 1)])
        ex = sb("ex", [P, 8 * (B + 1)])
        wt = sb("wt", [P, 2, B])
        nidx = sb("nidx", [P, 3, NB], I32)
        gidx = sb("gidx", [P, 3, KB], I32)
        indeg = sb("indeg", [P, NB])
        small = sb("small", [P, 12, 56])
        fixi = sb("fixi", [P, 4], I32)
        fixr = sb("fixr", [P, SMAX])
        fixm = sb("fixm", [P, 4, 8])
        fixk = sb("fixk", [P, 16])
        zrow = sb("zrow", [P, D])

        stage = rows[:, 0:KB * GMAX]
        nrow = rows[:, KB * GMAX:KB * (GMAX + SMAX)]
        o = KB * (GMAX + SMAX)
        xT = rows[:, o:o + KB * P]
        t1 = rows[:, o + KB * P:o + KB * P + KB * 136].rearrange("p (b d) -> p b d", d=136)
        t2 = rows[:, o + KB * (P + 136):o + KB * (P + 272)].rearrange("p (b d) -> p b d", d=136)
        zst = rows[:, o + KB * (P + 272):o + KB * (2 * P + 272)]
        hT = dstf[:, :, :, :].rearrange("p s b d -> p (s b d)")[:, 0:4 * KB * P].rearrange("p (c n) -> p c n", c=4)
        dflat = dstf[:, :, :, :].rearrange("p s b d -> p (s b d)")
        dsti = ebuf[:, 0:CH].bitcast(I32)
        dstF = ebuf[:, CH:2 * CH]
        sampb = ebuf[:, 2 * CH:3 * CH]
        junk = ebuf[:, 3 * CH:4 * CH]
        erow = ebuf[:, 4 * CH:4 * CH + KB * P].rearrange("p (b d) -> p b d", b=KB)
        tA = junk[:, 0:P]
        tB = junk[:, P:2 * P]
        coli = ebuf[:, 5 * CH:5 * CH + P].bitcast(I32)
        sflat = small[:, :, :].rearrange("p a b -> p (a b)")
        coarse = ebuf[:, 6 * CH:6 * CH + NB]
        fine = ebuf[:, 6 * CH + 64:6 * CH + 64 + NB]
        endf = ebuf[:, 6 * CH + 128:6 * CH + 128 + NB]
        begf = ebuf[:, 6 * CH + 192:6 * CH + 192 + NB]
        nodef = ebuf[:, 6 * CH + 256:6 * CH + 256 + NB]
        nodei = ebuf[:, 6 * CH + 320:6 * CH + 320 + NB].bitcast(I32)
        crsi = ebuf[:, 6 * CH + 384:6 * CH + 384 + NB].bitcast(I32)
        endT = ebuf[0:NB, 7 * CH:7 * CH + P]
        begT = ebuf[0:NB, 7 * CH + P:7 * CH + 2 * P]
        tmpm = ebuf[:, 7 * CH + 2 * P:7 * CH + 3 * P]
        tmp2 = ebuf[:, 7 * CH + 3 * P:7 * CH + 4 * P]
        keyf = ebuf[:, 4 * CH:5 * CH]
        highi = ebuf[:, 5 * CH:6 * CH].bitcast(I32)
        highf = junk
        lowf = sampb
        cnt = ebuf[:, 6 * CH + 448:6 * CH + 448 + NB]
        base = ebuf[:, 6 * CH + 512:6 * CH + 512 + NB]
        incl = ebuf[:, 6 * CH + 576:6 * CH + 576 + NB]
        cslast = ebuf[:, 6 * CH + 640:6 * CH + 644]
        LB = CH // 7
        lowT = rows[0:LB, 0:7 * P].rearrange("r (b c) -> r b c", b=7)
        ntile = B * P

        def hot(at, w):
            half = B * w // 2
            return rows[:, at:at + half].bitcast(BF16).rearrange("p (b w) -> p b w", b=B)

        hotL = [hot(s * ntile // 2, P) for s in range(2)]
        same = [hot(ntile + s * ntile // 2, P) for s in range(2)]
        hotH = [hot(2 * ntile + s * (B * NB // 2), NB) for s in range(2)]
        hotT = [sums[:, s * ntile:(s + 1) * ntile].rearrange("p (b w) -> p b w", b=B) for s in range(2)]
        cell = msg[:, 0:(B + 1) * NB].rearrange("p (b w) -> p b w", w=NB)
        picked = msg[:, (B + 1) * NB:(2 * B + 1) * NB].rearrange("p (b w) -> p b w", w=NB)
        sorted3 = rows[:, 0:CH * 3].rearrange("p (c k) -> p c k", k=3)
        chunkf = ebuf[:, 7 * CH + 4 * P:7 * CH + 4 * P + 8]

        psT = ctx.enter_context(nc.psum_tensor("psT", [P, 1024], F32))
        psM = ctx.enter_context(nc.psum_tensor("psM", [P, 4, 512], F32))
        psX = ctx.enter_context(nc.psum_tensor("psX", [P, 1024], F32))
        psMf = psM[:, :, :].rearrange("p a b -> p (a b)")
        mm256 = psMf[:, 0:KB * 256].rearrange("p (b d) -> p b d", d=256)
        mmX = psX[:, 0:KB * D].rearrange("p (b d) -> p b d", d=D)

        loaded = sem("loaded")
        attr_ready = sem("attr_ready")
        zeroed = sem("zeroed")
        zero_tile = sem("zero_tile")
        pool_const = sem("pool_const")
        consts = sem("consts")
        dst_saved = sem("dst_saved")
        sampled = sem("sampled")
        samples_in = sem("samples_in")
        search_ready = sem("search_ready")
        search_idx = sem("search_idx")
        search_rows = sem("search_rows")
        search_used = sem("search_used")
        ends_ready = sem("ends_ready")
        endsT_ready = sem("endsT_ready")
        ends_copied = sem("ends_copied")
        ends_saved = sem("ends_saved")
        begs_in = sem("begs_in")
        begs_T = sem("begs_T")
        diag_ready = sem("diag_ready")
        diag_done = sem("diag_done")
        first_ready = sem("first_ready")
        first_end = sem("first_end")
        index_ready = sem("index_ready")
        coarse_done = sem("coarse_done")
        keys_ready = sem("keys_ready")
        lowT_done = sem("lowT_done")
        lowT_copied = sem("lowT_copied")
        low_saved = sem("low_saved")
        hist_ready = sem("hist_ready")
        hist_used = sem("hist_used")
        hist_done = sem("hist_done")
        base_asked = sem("base_asked")
        base_sums = sem("base_sums")
        base_ready = sem("base_ready")
        place_ready = sem("place_ready")
        place_used = sem("place_used")
        sort_out = [sem(f"sort_out{s}") for s in range(2)]
        built = sem("built")
        prefix_done = sem("prefix_done")
        cell_ready = sem("cell_ready")
        ranks_done = sem("ranks_done")
        gate_ready = sem("gate_ready")
        msg_ready = sem("msg_ready")
        hold_step = sem("hold_step")
        acc_step = sem("acc_step")
        sorted_saved = sem("sorted_saved")
        sorted_in = sem("sorted_in")
        firstsrc_ready = sem("firstsrc_ready")
        ends1_ready = sem("ends1_ready")
        ends1_T = sem("ends1_T")
        ends1_copied = sem("ends1_copied")
        ends1_saved = sem("ends1_saved")
        first1_end = sem("first1_end")
        diag1_ready = sem("diag1_ready")
        diag1_done = sem("diag1_done")
        order_ready = sem("order_ready")
        low_landed = [sem(f"low_landed{s}") for s in range(2)]
        empty_rows = sem("empty_rows")
        dve_step = sem("dve_step")
        act_step = sem("act_step")
        pool_turn = sem("pool_turn")
        idx_staged = sem("idx_staged")
        rows_landed = [sem(f"rows_landed{s}") for s in range(2)]
        rows_used = sem("rows_used")
        dst_landed = [sem(f"dst_landed{s}") for s in range(2)]
        dst_used = sem("dst_used")
        attr_landed = [sem(f"attr_landed{s}") for s in range(2)]
        attr_turned = sem("attr_turned")
        attr_copied = sem("attr_copied")
        ebias_done = sem("ebias_done")
        ebias_kept = sem("ebias_kept")
        scores_ready = sem("scores_ready")
        weights_ready = sem("weights_ready")
        sums_ready = sem("sums_ready")
        sums_saved = [sem(f"sums_saved{s}") for s in range(2)]
        st_diag = sem("st_diag")
        st_max = sem("st_max")
        st_diff = sem("st_diff")
        st_exp = sem("st_exp")
        st_turn = sem("st_turn")
        st_copy = sem("st_copy")
        st_carry = sem("st_carry")
        fix_in = sem("fix_in")
        fix_pair = sem("fix_pair")
        fix_exp = sem("fix_exp")
        fix_ready = sem("fix_ready")
        fix_out = sem("fix_out")
        nidx_staged = sem("nidx_staged")
        nrow_in = sem("nrow_in")
        group_over = sem("group_over")
        nrow_used = sem("nrow_used")
        n_act = sem("n_act")
        n_actd = sem("n_actd")
        n_x = sem("n_x")
        n_t = sem("n_t")
        n_xT = sem("n_xT")
        n_mm = sem("n_mm")
        n_stage = sem("n_stage")
        n_ff = sem("n_ff")
        n_gelu = sem("n_gelu")
        n_ff2 = sem("n_ff2")
        tab_saved = sem("tab_saved")
        dtab_saved = sem("dtab_saved")
        scattered = sem("scattered")
        zfirst_in = sem("zfirst_in")
        zfirst_out = sem("zfirst_out")
        slim_in = sem("slim_in")
        slim_done = sem("slim_done")
        outp = sem("outp")

        def bb(name):
            return BIAS.index(name)

        def grp(it):
            return bass.ds(it * KB, KB)

        LOADS = 8 + len(BIAS) + 3 + 12 + 4
        block = ctx.enter_context(nc.Block())

        XS = [1, 1, 1, 3, 1, 0]
        ZW6 = ZW + [0]
        NAC = [0, 2, 2, 3, 1, 2]
        KD = [3, 26, 22, 36, 14, 17]
        MSG_PARTS = [1, 5, 9, 13]
        KE = [8, 18, 20, 18, 18]

        @block.sync
        def _(sp):
            n = [0]

            def load(dst_ap, src_ap):
                sp.dma_start(dst_ap, src_ap).then_inc(loaded, 16)
                n[0] += 1

            for q, by in ((search_used, 1), (nrow_used, 1), (group_over, 1), (tab_saved, 16), (dtab_saved, 16),
                          (rows_used, 2), (sums_saved[0], 16), (sums_saved[1], 16),
                          (dst_used, 1), (attr_turned, 2), (attr_copied, 1), (ebias_done, 1), (ebias_kept, 1),
                          (hist_used, 2), (built, 2), (place_used, 2)):
                sp.sem_inc(q, by)
            sp.wait_ge(zero_tile, 5)
            load(dsti[0:P - 1, :], a["dst"][0:(P - 1) * CH].rearrange("(p c) -> p c", c=CH))
            load(dsti[P - 1:P, 0:LASTV], a["dst"][(P - 1) * CH:E].rearrange("(p c) -> p c", p=1))
            load(X[:, 0:NB - 1, :], a["x"][0:(NB - 1) * P, :].rearrange("(b p) d -> p b d", p=P))
            load(X[0:ROWS, NB - 1, :], a["x"][(NB - 1) * P:N, :])
            load(src[0:P - 1, 0:CH], a["src"][0:(P - 1) * CH].rearrange("(p c) -> p c", c=CH))
            load(src[P - 1:P, 0:LASTV], a["src"][(P - 1) * CH:E].rearrange("(p c) -> p c", p=1))
            load(ew[0:P - 1, :], a["edge_weight"][0:(P - 1) * CH].rearrange("(p c) -> p c", c=CH))
            load(ew[P - 1:P, 0:LASTV], a["edge_weight"][(P - 1) * CH:E].rearrange("(p c) -> p c", p=1))
            for k, name in enumerate(BIAS):
                load(bias[:, k, :], a[name].rearrange("(o d) -> o d", o=1).to_broadcast([P, D]))
            load(beb[:, :], a["L2_gnn_be"].rearrange("(o d) -> o d", o=1).to_broadcast([P, 8]))
            load(b2b[:, :], a["L0_gnn_b2"].rearrange("(o d) -> o d", o=1).to_broadcast([P, 1]))
            load(b1c[:, :], a["L2_gnn_b1"])
            load(WA[0][:, 0:D], a["L0_gnn_W1"])
            load(WA[0][:, D:2 * D], a["L0_gnn_W4"])
            load(WA[1][:, 0:D], a["L1_gnn_W0"])
            load(WA[1][:, D:2 * D], a["L1_gnn_W1"])
            load(WA[2][:, 0:D], a["L2_gnn_Wq"])
            load(WA[2][:, D:2 * D], a["L2_gnn_Wk"])
            load(WA[3][:, 0:D], a["L3_gnn_W1"])
            load(WA[4][:, 0:D], a["L3_gnn_W2"])
            load(Wv[:, :], a["L2_gnn_Wv"])
            load(Wo[:, :], a["L2_gnn_Wo"])
            load(W1[:, :], a["L2_gnn_W1"])
            load(W2[:, :, :], a["L2_gnn_W2"].rearrange("(c p) n -> p c n", p=P))
            for k in range(4):
                load(Web[32 * k:32 * k + 32, 8 * k:8 * k + 8], a["L2_gnn_We"])
            assert n[0] == LOADS, n[0]

            sp.wait_ge(consts, 1)
            sp.dma_start(states_by_width[129][EP:EP + 1, :], sflat[0:1, 0:129]).then_inc(empty_rows, 16)
            sp.dma_start(states_by_width[144][EP:EP + 1, :], sflat[0:1, 0:144]).then_inc(empty_rows, 16)
            sp.dma_start(states_by_width[136][EP:EP + 1, :], sflat[0:1, 144:280]).then_inc(empty_rows, 16)

            sp.wait_ge(search_ready, 1)
            sp.dma_start(dst_rows.rearrange("r c -> (r c)").rearrange("(p c) -> p c", c=CH), dstF).then_inc(dst_saved, 16)
            sp.wait_ge(dst_saved, 16)
            sp.dma_start(samples.rearrange("(q r) -> q r", q=16),
                         dst_rows[:, 0:1].rearrange("(q r) c -> q (r c)", q=16), allow_slow_non_contiguous=True).then_inc(sampled, 16)
            sp.wait_ge(sampled, 16)
            sp.dma_start(sampb, samples.rearrange("(o r) -> o r", o=1).to_broadcast([P, BQ])).then_inc(samples_in, 16)

            wide = spread_wide.rearrange("(p c) d -> p c d", c=CH)
            sp.dma_start(spread_slim.rearrange("(p c) d -> p (c d)", c=CH), sums[:, 0:CH * 4]).then_inc(zeroed, 16)
            with sp.Fori(0, NG) as g:
                sp.dma_start(wide[:, bass.ds(g * B, B), :].rearrange("p b d -> p (b d)"),
                             msg[:, 0:B * D]).then_inc(zeroed, 16)
            sp.dma_start(attr_pad[E:EP, :].rearrange("(p r) d -> p (r d)", p=32), msg[0:32, 0:(EP - E) // 32 * 32]).then_inc(attr_ready, 16)
            sp.dma_start(attr_pad[0:E, :].rearrange("(q r) d -> q (r d)", q=160),
                         a["edge_attr_32"].rearrange("(q r) d -> q (r d)", q=160)).then_inc(attr_ready, 16)

            sp.wait_ge(ends_copied, 1)
            sp.dma_start(ends[0:1, :], zrow[0:1, 0:1]).then_inc(ends_saved, 16)
            sp.dma_start(ends[1:NP + 1, :].rearrange("(b p) o -> b (p o)", p=P), endT).then_inc(ends_saved, 16)
            sp.wait_ge(ends_saved, 32)
            sp.dma_start(begT, ends[0:NP, :].rearrange("(b p) o -> b (p o)", p=P)).then_inc(begs_in, 16)

            sp.wait_ge(lowT_copied, 1)
            sp.dma_start(low_rows.rearrange("(b r) c -> r b c", r=LB), lowT).then_inc(low_saved, 16)
            sp.wait_ge(low_saved, 16)
            low_all = low_rows.rearrange("r c -> (r c)").rearrange("(o n) -> o n", o=1)
            with sp.Fori(0, IT) as it:
                for s in range(2):
                    g = it * 2 + s
                    sp.wait_ge(built, g + 1)
                    sp.dma_start(dstf[:, s, :, :].rearrange("p b c -> p (b c)"),
                                 low_all[:, bass.ds(g * ntile, ntile)].to_broadcast([P, ntile])).then_inc(low_landed[s], 16)
            for s in range(2):
                sp.wait_ge(sort_out[s], 16 * B * IT)
            sp.dma_start(rows[:, 0:CH * 3], by_src.rearrange("(p c) k -> p (c k)", c=CH)).then_inc(sorted_in, 16)
            sp.wait_ge(ends1_copied, 1)
            sp.dma_start(ends_src.rearrange("(b p) o -> b (p o)", p=P), endT).then_inc(ends1_saved, 16)

            tab = Steps(n_stage)
            for ph in range(6):
                if ph < 5:
                    with sp.Fori(0, KG) as it:
                        tab.loop(it, 1)
                        tab.add()
                        sp.wait_ge(n_stage, tab.value())
                        sp.dma_start(table[ph].rearrange("(b p) w -> p b w", p=P)[:, grp(it), :],
                                     stage[:, 0:KB * GW[ph]].rearrange("p (b w) -> p b w", b=KB)).then_inc(tab_saved, 16)
                        if ZW[ph]:
                            sp.dma_start(dst_table[ph].rearrange("(b p) w -> p b w", p=P)[:, grp(it), :],
                                         zst[:, 0:KB * ZW[ph]].rearrange("p (b w) -> p b w", b=KB)).then_inc(dtab_saved, 16)
                    tab.close(KG)
                else:
                    with sp.Fori(0, KG - 1) as it:
                        tab.loop(it, 1)
                        tab.add()
                        sp.wait_ge(n_stage, tab.value())
                        sp.dma_start(out[0:(NB - 1) * P, :].rearrange("(b p) w -> p b w", p=P)[:, grp(it), :],
                                     X[:, grp(it), :]).then_inc(outp, 16)
                    tab.close(KG - 1)
                    tab.add()
                    sp.wait_ge(n_stage, tab.value())
                    sp.dma_start(out[(NB - KB) * P:(NB - 1) * P, :].rearrange("(b p) w -> p b w", p=P),
                                 X[:, NB - KB:NB - 1, :]).then_inc(outp, 16)
                    sp.dma_start(out[(NB - 1) * P:N, :], X[0:ROWS, NB - 1, :]).then_inc(outp, 16)
                    sp.wait_ge(outp, 16 * (KG + 1))
                    continue
                if ZW[ph]:
                    done = [0, 2, 3, 4].index(ph) + 1
                    view = spread[ph].rearrange("(p c) d -> p c d", c=CH)
                    sp.wait_ge(zfirst_in, 16 * done)
                    sp.wait_ge(scattered, 16 * NB * done)
                    sp.dma_start(view[:, 0, :], zrow[:, 0:ZW[ph]]).then_inc(zfirst_out, 16)
                    sp.wait_ge(zfirst_out, 16 * done)
                    if ZW[ph] == 4:
                        sp.wait_ge(tab_saved, 16 + 16 * KG * (ph + 1))
                        sp.wait_ge(dtab_saved, 16 + 16 * KG * done)
                        sp.dma_start(rows[:, 0:CH * 4], view.rearrange("p c d -> p (c d)")).then_inc(slim_in, 16)
                if ZW[ph] == D:
                    q = 1 + [0, 2].index(ph) * NG
                    with sp.Fori(0, IT) as it:
                        for s in range(2):
                            g = it * 2 + s
                            sp.wait_ge(dst_used, g + q)
                            sp.dma_start(dstf[:, s, :, :].rearrange("p b d -> p (b d)"),
                                         view[:, bass.ds(g * B, B), :].rearrange("p b d -> p (b d)")).then_inc(dst_landed[s], 16)
                if ph == 1:
                    sp.wait_ge(attr_ready, 32)
                    with sp.Fori(0, IT) as it:
                        for s in range(2):
                            g = it * 2 + s
                            sp.wait_ge(attr_turned, g + 1)
                            sp.dma_start(attr[:, s, :],
                                         attr_pad.rearrange("(p c) d -> p (c d)", c=CH)[:, bass.ds(g * (B * 32), B * 32)]).then_inc(attr_landed[s], 16)

        @block.gpsimd
        def _(pool):
            pool.memset(src[:, :], N).then_inc(zero_tile, 1)
            pool.memset(ew[:, :], 0.0).then_inc(zero_tile, 1)
            pool.memset(dsti, N).then_inc(zero_tile, 1)
            pool.memset(Web[:, :], 0.0).then_inc(zero_tile, 1)
            pool.memset(X[:, NB - 1, :], 0.0).then_inc(zero_tile, 1)
            pool.iota(nodei, pattern=[[P, NB]], base=0, channel_multiplier=1).then_inc(pool_const, 1)
            pool.memset(ident[:, :], 0.0).then_inc(pool_const, 1)
            pool.memset(ones[:, :], 1.0).then_inc(pool_const, 1)
            pool.iota(coli, pattern=[[1, P]], base=0, channel_multiplier=0).then_inc(pool_const, 1)
            pool.iota(fixi[:, 0:2], pattern=[[0, 2]], base=CH, channel_multiplier=CH).then_inc(pool_const, 1)
            pool.wait_ge(pool_const, 5)
            pool.affine_select(out=ident[:, :], in_=ident[:, :], compare_op=ALU.not_equal, fill=1.0, base=0,
                               pattern=[[-1, P]], channel_multiplier=1).then_inc(pool_const, 1)
            pool.affine_select(out=tmpm, in_=ones[:, :], compare_op=ALU.is_gt, fill=0.0, base=0,
                               pattern=[[1, P]], channel_multiplier=-1).then_inc(pool_const, 1)
            pool.affine_select(out=tmp2, in_=ones[:, :], compare_op=ALU.is_gt, fill=0.0, base=0,
                               pattern=[[-1, P]], channel_multiplier=1).then_inc(pool_const, 1)

            turns = Steps(pool_turn)
            with pool.Fori(0, KG) as it:
                pool.wait_ge(search_idx, it + 1)
                pool.sem_inc(pool_turn, 1)
                for b in range(KB):
                    pool.indirect_dma_start(erow[:, b, :], None, dst_rows[:, :],
                                            bass.IndirectOffsetOnAxis(ap=gidx[:, 0, b:b + 1], axis=0)).then_inc(search_rows, 16)
            pool.wait_ge(first_ready, 1)
            pool.wait_ge(ends_saved, 32)
            pool.indirect_dma_start(fixr[:, 0:1], None, ends[:, :],
                                    bass.IndirectOffsetOnAxis(ap=fixi[:, 1:2], axis=0)).then_inc(first_end, 16)
            def scatter_turn(it, first=False):
                for s in range(2):
                    g = it * 2 + s
                    pool.wait_ge(place_ready, g + 1)
                    pool.sem_inc(pool_turn, 1)
                    for j in range(B):
                        pool.indirect_dma_start(by_src[:, :], bass.IndirectOffsetOnAxis(ap=place[:, s, j:j + 1], axis=0),
                                                payload[:, s, j, :], None).then_inc(sort_out[s], 16)
                    if s or not first:
                        pool.wait_ge(sort_out[1 - s], (it + s) * (16 * B))
                        pool.sem_inc(place_used, 1)

            scatter_turn(0, first=True)
            with pool.Fori(1, IT) as it:
                scatter_turn(it)
            pool.wait_ge(firstsrc_ready, 1)
            pool.wait_ge(ends1_saved, 16)
            pool.indirect_dma_start(fixr[:, 0:1], None, ends_src[:, :],
                                    bass.IndirectOffsetOnAxis(ap=fixi[:, 2:3], axis=0)).then_inc(first1_end, 16)
            pool.wait_ge(order_ready, 1)
            staged = Steps(n_stage)
            used = Steps(nrow_used, 1)
            nix = Steps(nidx_staged)
            for ph in range(6):
                if ph == 0:
                    pool.wait_ge(zeroed, 16 * (NG + 1))
                if ph == 1:
                    pool.wait_ge(empty_rows, 48)
                with pool.Fori(0, KG) as it:
                    staged.loop(it, 1)
                    used.loop(it, 1)
                    nix.loop(it, 1)
                    nix.add()
                    pool.wait_ge(nidx_staged, nix.value())
                    pool.sem_inc(pool_turn, 1)
                    if ph > 0:
                        p = ph - 1
                        pool.wait_ge(nrow_used, used.value())
                        pool.sem_inc(pool_turn, 1)
                        for b in range(KB):
                            pool.indirect_dma_start(nrow[:, b * SW[p]:(b + 1) * SW[p]], None, states[p][:, :],
                                                    bass.IndirectOffsetOnAxis(ap=gidx[:, 2 if p == 1 else 0, b:b + 1], axis=0)).then_inc(nrow_in, 16)
                        used.add()
                    staged.add()
                    if ph in (0, 2, 3, 4):
                        pool.wait_ge(n_stage, staged.value())
                        pool.sem_inc(pool_turn, 1)
                        for b in range(KB):
                            pool.indirect_dma_start(spread[ph][:, :], bass.IndirectOffsetOnAxis(ap=gidx[:, 1, b:b + 1], axis=0),
                                                    zst[:, b * ZW[ph]:(b + 1) * ZW[ph]], None,
                                                    bounds_check=EP - 1, oob_is_err=False).then_inc(scattered, 16)
                        pool.wait_ge(scattered, it * (16 * KB) + (16 * KB + 16 * NB * [0, 2, 3, 4].index(ph)))
                    if ph > 0:
                        pool.wait_ge(nrow_in, it * (16 * KB) + (16 * KB + 16 * NB * (ph - 1)))
                    pool.sem_inc(group_over, 1)
                staged.close(KG)
                nix.close(KG)
                if ph > 0:
                    used.close(KG)
                if ph == 5:
                    continue
                if ZW[ph]:
                    nz = [0, 2, 3, 4].index(ph)
                    pool.wait_ge(dtab_saved, 16 + 16 * KG * (nz + 1))
                    if nz:
                        pool.wait_ge(zfirst_out, 16 * nz)
                    pool.indirect_dma_start(zrow[:, 0:ZW[ph]], None, dst_table[ph][:, :],
                                            bass.IndirectOffsetOnAxis(ap=fixi[:, 0:1], axis=0)).then_inc(zfirst_in, 16)
                pool.wait_ge(tab_saved, 16 + 16 * KG * (ph + 1))
                if ZW[ph] == 4:
                    pool.wait_ge(slim_done, ph - 2)
                if ZW[ph]:
                    pool.wait_ge(scattered, 16 * NB * (nz + 1))
                with pool.Fori(0, IT) as it:
                    for s in range(2):
                        g = it * 2 + s
                        pool.wait_ge(idx_staged, g + (1 + ph * (NG + 2)))
                        pool.sem_inc(pool_turn, 1)
                        pool.wait_ge(rows_used, g + (1 + ph * NG))
                        pool.sem_inc(pool_turn, 1)
                        for j in range(B):
                            at = (s * B + j) * GW[ph]
                            pool.indirect_dma_start(rows[:, at:at + GW[ph]], None, table[ph][:, :],
                                                    bass.IndirectOffsetOnAxis(ap=idx[:, s, j:j + 1], axis=0)).then_inc(rows_landed[s], 16)
                for s in range(2):
                    pool.wait_ge(sums_saved[s], 16 + 16 * IT * (ph + 1))
                k = 2 if ph == 1 else 1
                pool.indirect_dma_start(fixr[:, 0:SW[ph]], None, states[ph][:, :],
                                        bass.IndirectOffsetOnAxis(ap=fixi[:, k:k + 1], axis=0)).then_inc(fix_in, 16)
                pool.wait_ge(fix_ready, ph + 1)
                pool.indirect_dma_start(states[ph][:, :], bass.IndirectOffsetOnAxis(ap=fixi[:, k:k + 1], axis=0),
                                        fixr[:, 0:SW[ph]], None).then_inc(fix_out, 16)
                pool.wait_ge(fix_out, 16 * (ph + 1))

        @block.tensor
        def _(pe):
            def turn(blocks, src_of):
                for b in range(blocks):
                    last = pe.transpose(psT[:, b * P:(b + 1) * P], src_of(b), ident[:, :])
                return last

            pe.wait_ge(pool_const, 8)
            pe.wait_ge(loaded, 16 * LOADS)
            pe.wait_ge(consts, 1)
            pe.wait_ge(diag_ready, 1)
            pe.matmul(psX[:, 0:P], ones[:, :], tA, start=True, stop=True)
            pe.matmul(psX[:, P:2 * P], ones[:, :], tB, start=True, stop=True).then_inc(diag_done, 1)
            pe.wait_ge(ends_ready, 1)
            pe.transpose(psT[0:NB, 0:P], endf, ident[:, :]).then_inc(endsT_ready, 1)
            pe.wait_ge(begs_in, 16)
            pe.wait_ge(ends_copied, 1)
            pe.transpose(psT[:, 512:512 + NB], begT, ident[0:NB, 0:NB]).then_inc(begs_T, 1)
            pe.wait_ge(index_ready, 1)

            pe.wait_ge(keys_ready, 1)
            for b in range(7):
                m = pe.transpose(psT[0:LB, b * P:(b + 1) * P], lowf[:, b * LB:(b + 1) * LB], ident[:, :])
            m.then_inc(lowT_done, 1)
            cells = psM[:, 0, 0:NB]
            pe.wait_ge(lowT_copied, 1)
            pe.wait_ge(low_saved, 16)
            pe.matmul(cells, ident[:, :], zrow[:, 0:NB], start=True, stop=True)
            with pe.Fori(0, IT) as it:
                for s in range(2):
                    g = it * 2 + s
                    pe.wait_ge(hist_ready, g + 1)
                    for j in range(B):
                        m = pe.matmul(cells, hotL[s][:, j, :], hotH[s][:, j, :], start=False, stop=True, skip_group_check=True)
                    m.then_inc(hist_used, 1)
            pe.matmul(cells, ident[:, :], zrow[:, 0:NB], start=False, stop=True, skip_group_check=True).then_inc(hist_done, 1)
            pe.wait_ge(base_asked, 1)
            pe.matmul(psX[:, 0:NB], tmpm, cnt, start=True, stop=True)
            pe.matmul(psX[:, 64:64 + NB], ones[:, :], cnt, start=True, stop=True).then_inc(base_sums, 1)
            pe.wait_ge(base_ready, 1)

            def prefixes(s):
                for i in range(B):
                    for k in range(2):
                        lo = max(i, 7 * k)
                        if lo < 7 * k + 7:
                            m = pe.matmul(psM[:, k, (lo - 7 * k) * NB:7 * NB].rearrange("p (c w) -> p c w", w=NB), hotL[s][:, i, :],
                                          hotH[s][:, i, :].unsqueeze(1).to_broadcast([P, 7 * k + 7 - lo, NB]),
                                          start=(i == 0), stop=(i == 7 * k + 6))
                m.then_inc(prefix_done, 1)

            def rank_turn(it, last=False):
                for s in range(2):
                    g = it * 2 + s
                    pe.wait_ge(cell_ready, g + 1)
                    for j in range(B):
                        t = psX[:, j // 7 * 512 + j % 7 * NB:j // 7 * 512 + (j % 7 + 1) * NB]
                        pe.matmul(t, hotT[s][:, j, :], cell[:, j, :], start=True, stop=False)
                        m = pe.matmul(t, same[s][:, j, :], hotH[s][:, j, :], start=False, stop=True)
                    m.then_inc(ranks_done, 1)
                    if not (last and s):
                        pe.wait_ge(built, g + 4)
                        prefixes(1 - s)

            pe.wait_ge(built, 3)
            prefixes(0)
            with pe.Fori(0, IT - 1) as it:
                rank_turn(it)
            rank_turn(IT - 1, last=True)
            pe.wait_ge(diag1_ready, 1)
            pe.matmul(psX[:, 0:P], ones[:, :], tA, start=True, stop=True)
            pe.matmul(psX[:, P:2 * P], ones[:, :], tB, start=True, stop=True).then_inc(diag1_done, 1)
            pe.wait_ge(ends1_ready, 1)
            pe.transpose(psT[0:NB, 0:P], endf, ident[:, :]).then_inc(ends1_T, 1)
            pe.wait_ge(order_ready, 1)

            x = Steps(n_x)
            xt = Steps(n_xT)
            gel = Steps(n_gelu)
            for ph in range(5):
                with pe.Fori(0, KG) as it:
                    per = XS[ph]
                    x.loop(it, per)
                    xt.loop(it, per)
                    gel.loop(it, 2)
                    if ph == 3:
                        x.add()
                        pe.wait_ge(n_x, x.value())
                        turn(KB, lambda b: t1[:, b, 0:D]).then_inc(n_t, 1)
                        xt.add()
                        pe.wait_ge(n_xT, xt.value())
                        for b in range(KB):
                            m = pe.matmul(mmX[:, b, :], xT[:, b * P:(b + 1) * P], Wo[:, :], start=True, stop=True)
                        m.then_inc(n_mm, 1)
                        x.add()
                        pe.wait_ge(n_x, x.value())
                        turn(KB, lambda b: t2[:, b, 0:D]).then_inc(n_t, 1)
                        xt.add()
                        pe.wait_ge(n_xT, xt.value())
                        for half in range(2):
                            if half:
                                gel.add()
                                pe.wait_ge(n_gelu, gel.value())
                            for c in range(2):
                                for q in range(2):
                                    m = pe.matmul(psM[:, c * 2 + q, 0:448], W1[:, (half * 2 + c) * P:(half * 2 + c + 1) * P],
                                                  xT[:, q * 448:(q + 1) * 448], start=True, stop=True)
                            m.then_inc(n_ff, 1)
                        gel.add()
                        pe.wait_ge(n_gelu, gel.value())
                        for b in range(KB):
                            for c in range(4):
                                m = pe.matmul(mmX[:, b, :], hT[:, c, b * P:(b + 1) * P], W2[:, c, :], start=(c == 0), stop=(c == 3))
                        m.then_inc(n_ff2, 1)
                    x.add()
                    pe.wait_ge(n_x, x.value())
                    turn(KB, lambda b: t1[:, b, 0:D]).then_inc(n_t, 1)
                    xt.add()
                    pe.wait_ge(n_xT, xt.value())
                    w = 256 if ph < 3 else 136
                    for b in range(KB):
                        m = pe.matmul(mm256[:, b, 0:w], xT[:, b * P:(b + 1) * P], WA[ph][:, :], start=True, stop=True)
                        if ph == 2:
                            m = pe.matmul(mmX[:, b, :], xT[:, b * P:(b + 1) * P], Wv[:, :], start=True, stop=True)
                    m.then_inc(n_mm, 1)
                x.close(KG)
                xt.close(KG)
                if ph == 3:
                    gel.close(KG)
                if ph == 1:
                    with pe.Fori(0, IT) as it:
                        for s in range(2):
                            g = it * 2 + s
                            pe.wait_ge(attr_landed[s], it * 16 + 16)
                            pe.wait_ge(attr_copied, g + 1)
                            for q in range(4):
                                w = P if q < 3 else 64
                                m = pe.transpose(psT[0:w, q * P:(q + 1) * P], attr[:, s, q * P:q * P + w], ident[:, :])
                            m.then_inc(attr_turned, 1)
                            pe.wait_ge(attr_copied, g + 2)
                            pe.wait_ge(ebias_kept, g + 1)
                            for q in range(4):
                                w = P if q < 3 else 64
                                m = pe.matmul(psX[:, q * 32:q * 32 + w // 4], attrT[0:w, q * P:(q + 1) * P], Web[0:w, 0:w // 4],
                                              start=True, stop=True)
                            m.then_inc(ebias_done, 1)
                H, F, d1 = HEADS[ph], FW[ph], HD1[ph]
                last = sums[:, (B + B - 1) * SW[ph]:2 * B * SW[ph]]
                pe.wait_ge(sums_ready, NG * (ph + 1))
                if ph == 0:
                    pe.matmul(psX[:, 0:F], chains[0][:, :], last[:, 0:F], start=True, stop=True).then_inc(st_carry, 1)
                    continue
                pe.wait_ge(st_diag, ph)
                for k in range(H // 4):
                    m = pe.matmul(psM[:, k, :], ones[:, :], dflat[:, k * 512:(k + 1) * 512], start=True, stop=True)
                m.then_inc(st_max, 1)
                pe.wait_ge(st_exp, ph)
                for h in range(H):
                    m = pe.transpose(psM[:, 2 + h // 4, h % 4 * P:(h % 4 + 1) * P], dflat[:, 1024 + h * P:1024 + (h + 1) * P], ident[:, :])
                m.then_inc(st_turn, 1)
                pe.wait_ge(st_copy, ph)
                for h in range(H):
                    m = pe.matmul(psX[:, h * d1:(h + 1) * d1], dflat[:, 2048 + h * P:2048 + (h + 1) * P],
                                  last[:, h * d1:(h + 1) * d1], start=True, stop=True)
                m.then_inc(st_carry, 1)

        @block.scalar
        def _(act):
            step = Steps(act_step)
            used = Steps(search_used, 1)
            act.wait_ge(coarse_done, 1)
            with act.Fori(0, KG) as it:
                used.loop(it, 1)
                act.wait_ge(search_used, used.value())
                act.sem_inc(act_step, 1)
                act.activation(gidx[:, 0, :], crsi[:, grp(it)], ACT.Copy).then_inc(search_idx, 1)
                used.add()
            used.close(KG)
            act.wait_ge(endsT_ready, 1)
            act.activation(endT, psT[0:NB, 0:P], ACT.Copy).then_inc(ends_copied, 1)
            act.wait_ge(index_ready, 1)

            act.wait_ge(lowT_done, 1)
            act.activation(lowT[:, 0:4, :].rearrange("r b c -> r (b c)"), psT[0:LB, 0:512], ACT.Copy)
            act.activation(lowT[:, 4:7, :].rearrange("r b c -> r (b c)"), psT[0:LB, 512:7 * P], ACT.Copy).then_inc(lowT_copied, 1)
            act.wait_ge(ends1_T, 1)
            act.activation(endT, psT[0:NB, 0:P], ACT.Copy).then_inc(ends1_copied, 1)
            act.wait_ge(order_ready, 1)

            t = Steps(n_t)
            aq = Steps(n_act)
            ff = Steps(n_ff)
            for ph in range(6):
                with act.Fori(0, KG) as it:
                    act.wait_ge(group_over, it + (1 + KG * ph))
                    act.sem_inc(act_step, 1)
                    act.activation(gidx[:, :, :], nidx[:, :, grp(it)], ACT.Copy).then_inc(nidx_staged, 1)
                    t.loop(it, XS[ph])
                    aq.loop(it, NAC[ph])
                    ff.loop(it, 2)

                    def turned():
                        t.add()
                        act.wait_ge(n_t, t.value())
                        act.activation(xT[:, 0:512], psT[:, 0:512], ACT.Copy)
                        act.activation(xT[:, 512:KB * P], psT[:, 512:KB * P], ACT.Copy).then_inc(n_xT, 1)

                    def call(o_ap, i_ap, f, **kw):
                        aq.add()
                        act.wait_ge(n_act, aq.value())
                        act.activation(o_ap, i_ap, f, **kw).then_inc(n_actd, 1)

                    def root(k, n, e):
                        call(small[:, k, 0:n], small[:, k, 0:n], ACT.Sqrt, scale=1.0, bias=eps[:, e:e + 1])

                    if ph == 1:
                        root(1, KB, 0)
                    if ph == 2:
                        root(1, 28, 1)
                        root(1, KB, 0)
                    if ph == 3:
                        turned()
                        root(1, KB, 0)
                        turned()
                        for half in range(2):
                            ff.add()
                            act.wait_ge(n_ff, ff.value())
                            for c in range(2):
                                for q in range(2):
                                    m = act.activation(hT[:, half * 2 + c, q * 448:(q + 1) * 448], psM[:, c * 2 + q, 0:448], ACT.Gelu,
                                                       scale=1.0, bias=b1c[:, half * 2 + c:half * 2 + c + 1])
                            m.then_inc(n_gelu, 1)
                        root(1, KB, 0)
                        root(1, KB, 0)
                        turned()
                    if ph in (4, 5):
                        call(small[:, 4, 0:56], small[:, 3, 0:56], ACT.Exp)
                    if ph == 5:
                        root(1, KB, 0)
                    if ph in (0, 1, 2, 4):
                        turned()
                    if ph == 1:
                        root(1, 28, 1)
                aq.close(KG)
                if ph < 5:
                    t.close(KG)
                else:
                    continue
                if ph == 3:
                    ff.close(KG)
                H, d1, F, W = HEADS[ph], HD1[ph], FW[ph], SW[ph]
                act.wait_ge(rows_used, 2 + ph * NG)
                source = src1 if ph == 1 else src
                for s in range(2):
                    act.activation(idx[:, s, :], source[:, s * B:(s + 1) * B], ACT.Copy).then_inc(idx_staged, 1)
                with act.Fori(0, IT) as it:
                    for s in range(2):
                        g = it * 2 + s
                        if ph == 1:
                            act.wait_ge(attr_turned, g + 3)
                            act.sem_inc(act_step, 1)
                            act.activation(attrT[:, 0:3 * P], psT[:, 0:3 * P], ACT.Copy)
                            act.activation(attrT[0:64, 3 * P:4 * P], psT[0:64, 3 * P:4 * P], ACT.Copy).then_inc(attr_copied, 1)
                        act.wait_ge(scores_ready, g + (1 + ph * NG))
                        if ph == 0:
                            act.activation(ex[:, s * B:(s + 1) * B], ex[:, s * B:(s + 1) * B], ACT.Exp, scale=-1.0, bias=b2b[:, 0:1]).then_inc(gate_ready, 1)
                            act.wait_ge(weights_ready, g + 1)
                            act.sem_inc(act_step, 1)
                            for j in range(B):
                                at = (s * B + j) * GW[0] + D
                                m = act.activation(msg[:, j * F:(j + 1) * F], rows[:, at:at + F], ACT.Copy, scale=wt[:, s, j:j + 1])
                                if j in MSG_PARTS[:-1]:
                                    m.then_inc(msg_ready, 1)
                            m.then_inc(rows_used, 1)
                        else:
                            n = H * (B + 1)
                            act.activation(ex[:, 0:n], df[:, 0:n], ACT.Exp).then_inc(weights_ready, 1)
                        act.wait_ge(rows_used, g + (3 + ph * NG))
                        act.sem_inc(act_step, 1)
                        act.activation(idx[:, s, :], source[:, bass.ds((g + 2) * B, B)], ACT.Copy).then_inc(idx_staged, 1)
                        act.wait_ge(sums_ready, g + (1 + ph * NG))
                        act.dma_start(states[ph][0:EP, :].rearrange("(p c) w -> p c w", c=CH)[:, bass.ds(g * B, B), :].rearrange("p b w -> p (b w)"),
                                      sums[:, s * B * W:(s + 1) * B * W]).then_inc(sums_saved[s], 16)
                if ph == 0:
                    continue
                act.wait_ge(st_diff, ph)
                act.activation(dflat[:, 1024:1024 + H * P], dflat[:, 1024:1024 + H * P], ACT.Exp).then_inc(st_exp, 1)
                act.wait_ge(st_turn, ph)
                for k in range(H // 4):
                    m = act.activation(dflat[:, 2048 + k * 512:2048 + (k + 1) * 512], psM[:, 2 + k, :], ACT.Copy)
                m.then_inc(st_copy, 1)
                act.wait_ge(fix_pair, ph)
                act.activation(fixm[:, 2:4, 0:H], fixm[:, 0:2, 0:H], ACT.Exp).then_inc(fix_exp, 1)

        @block.vector
        def _(dve):
            st = Steps(dve_step)

            def link(ins):
                ins.then_inc(dve_step, 1)
                st.add()
                dve.wait_ge(dve_step, st.value())

            def tell(ins, steps):
                ins.then_inc(steps.sem, 1)
                steps.add()
                dve.wait_ge(steps.sem, steps.value())

            def tt(o_, a_, b_, op):
                return dve.tensor_tensor(o_, a_, b_, op)

            def ts(o_, a_, s1, op0, s2=None, op1=None):
                if op1 is None:
                    return dve.tensor_scalar(o_, a_, s1, None, op0)
                return dve.tensor_scalar(o_, a_, s1, s2, op0, op1)

            def cp(o_, a_):
                return dve.tensor_scalar(o_, a_, 1.0, None, ALU.mult)

            def stt(o_, a_, s_, b_, op0, op1):
                return dve.scalar_tensor_tensor(o_, a_, s_, b_, op0, op1)

            def red(o_, a_, op=ALU.add):
                return dve.tensor_reduce(o_, a_, AX.X, op)

            link(dve.memset(sums[:, :], 0.0))
            link(dve.memset(msg[:, :], 0.0))
            link(dve.memset(zrow[:, :], 0.0))
            link(dve.memset(eps[:, 0:1], 1e-5))
            link(dve.memset(eps[:, 1:2], 1e-9))
            link(dve.memset(nf[:, :], -BIG))
            link(dve.memset(sflat[:, 0:280], 0.0))
            link(dve.memset(sflat[:, 136:144], -BIG))
            dve.memset(sflat[:, 276:280], -BIG).then_inc(consts, 1)
            dve.wait_ge(consts, 1)
            dve.wait_ge(loaded, 16 * LOADS)
            dve.wait_ge(pool_const, 8)
            link(ts(b2b[:, :], b2b[:, :], -1.0, ALU.mult))
            dve.tensor_copy(dstF, dsti).then_inc(search_ready, 1)
            dve.wait_ge(search_ready, 1)
            link(dve.tensor_copy(nodef, nodei))
            link(ts(tA, ident[:, :], dstF[:, 0:1], ALU.mult))
            dve.tensor_scalar(tB, ident[:, :], dstF[:, CH - 1:CH], None, ALU.mult).then_inc(diag_ready, 1)
            link(dve.tensor_copy(chunkf[:, 0:1], fixi[:, 0:1]))
            link(dve.tensor_copy(fixi[:, 0:1], dstF[:, 0:1]))
            dve.tensor_scalar(fixi[:, 1:2], dstF[:, 0:1], 1.0, None, ALU.add).then_inc(first_ready, 1)
            link(dve.memset(cont[:, 0:1], 0.0))
            link(tt(cont[:, 1:CH], dstF[:, 1:CH], dstF[:, 0:CH - 1], ALU.is_equal))
            link(dve.tensor_copy(colf[:, :], coli))

            def chain_masks(k, first, last):
                link(stt(chains[k][:, :], psX[:, 0:P], last, tmpm, ALU.is_equal, ALU.mult))
                link(stt(fars[k][:, :], psX[:, P:2 * P], first, tmp2, ALU.is_equal, ALU.mult))
                link(ts(fars[k][:, :], fars[k][:, :], -1.0, ALU.add, BIG, ALU.mult))

            dve.wait_ge(diag_done, 1)
            chain_masks(0, dstF[:, 0:1], dstF[:, CH - 1:CH])
            for p, (ks, kd) in ((3, ("L3_gnn_a_src1", "L3_gnn_a_dst1")), (4, ("L3_gnn_a_src2", "L3_gnn_a_dst2"))):
                for k, name in enumerate((ks, kd)):
                    link(tt(junk[:, 256:384], WA[p][:, 0:D], bias[:, bb(name), :], ALU.mult))
                    link(red(WA[p][:, D + 4 * k:D + 4 * k + 4], junk[:, 256:384].rearrange("p (h d) -> p h d", h=4)))

            dve.wait_ge(samples_in, 16)
            with dve.Fori(0, NB) as b:
                st.loop(b, 1)
                link(dve.tensor_scalar(junk, sampb, nodef[:, bass.ds(b, 1)], 0.0, ALU.is_le, ALU.add,
                                       accum_out=coarse[:, bass.ds(b, 1)]))
            st.close(NB)
            link(ts(coarse, coarse, -1.0, ALU.add, 0.0, ALU.max))
            dve.tensor_copy(crsi, coarse).then_inc(coarse_done, 1)
            use = Steps(search_used, 1)
            with dve.Fori(0, KG) as it:
                use.loop(it, 1)
                st.loop(it, KB - 1)
                dve.wait_ge(search_rows, it * (16 * KB) + 16 * KB)
                for b in range(KB):
                    m = dve.tensor_scalar(junk[:, 0:P], erow[:, b, :], nodef[:, bass.ds(it * KB + b, 1)], 0.0, ALU.is_le, ALU.add,
                                          accum_out=fine[:, bass.ds(it * KB + b, 1)])
                    if b < KB - 1:
                        link(m)
                    else:
                        tell(m, use)
            use.close(KG)
            st.close(KG)
            dve.scalar_tensor_tensor(endf, coarse, float(P), fine, ALU.mult, ALU.add).then_inc(ends_ready, 1)
            dve.wait_ge(ends_ready, 1)
            dve.wait_ge(begs_T, 1)
            link(dve.tensor_copy(begf, psT[:, 512:512 + NB]))
            link(tt(indeg[:, :], endf, begf, ALU.subtract))
            has = junk[:, 0:NB]
            scr = junk[:, 64:64 + NB]
            link(ts(has, indeg[:, :], 0.0, ALU.is_gt))
            link(stt(scr, endf, float(-1 - EP), has, ALU.add, ALU.mult))
            link(ts(nidx[:, 0, :], scr, float(EP), ALU.add))
            link(ts(has, has, float(-EP), ALU.mult, float(EP), ALU.add))
            link(tt(nidx[:, 1, :], has, begf, ALU.add))
            dve.wait_ge(first_end, 16)
            link(tt(chunkf[:, 1:2], fixr[:, 0:1], chunkf[:, 0:1], ALU.min))
            dve.tensor_scalar(fixi[:, 1:2], chunkf[:, 1:2], -1.0, None, ALU.add).then_inc(index_ready, 1)
            dve.wait_ge(index_ready, 1)

            link(ts(highi, src[:, 0:CH], 7, ALU.arith_shift_right))
            link(dve.tensor_copy(highf, highi))
            link(dve.tensor_copy(keyf, src[:, 0:CH]))
            dve.scalar_tensor_tensor(lowf, highf, float(-P), keyf, ALU.mult, ALU.add).then_inc(keys_ready, 1)
            dve.wait_ge(keys_ready, 1)
            dve.wait_ge(low_saved, 16)
            with dve.Fori(0, IT) as it:
                for s in range(2):
                    g = it * 2 + s
                    ce = bass.ds(g * B, B)
                    dve.wait_ge(hist_used, g + 1)
                    tt(hotL[s], lowf[:, ce].unsqueeze(2).to_broadcast([P, B, P]), colf[:, :].unsqueeze(1).to_broadcast([P, B, P]), ALU.is_equal)
                    tt(hotH[s], highf[:, ce].unsqueeze(2).to_broadcast([P, B, NB]), colf[:, 0:NB].unsqueeze(1).to_broadcast([P, B, NB]),
                       ALU.is_equal).then_inc(hist_ready, 1)
            dve.wait_ge(hist_done, 1)
            dve.tensor_copy(cnt, psM[:, 0, 0:NB]).then_inc(base_asked, 1)
            dve.wait_ge(base_asked, 1)
            dve.wait_ge(base_sums, 1)
            link(dve.tensor_tensor_scan(incl, ones[:, 0:NB], psX[:, 64:64 + NB], 0.0, ALU.mult, ALU.add))
            link(tt(incl, incl, psX[:, 64:64 + NB], ALU.subtract))
            dve.tensor_tensor(base, incl, psX[:, 0:NB], ALU.add).then_inc(base_ready, 1)
            dve.wait_ge(base_ready, 1)

            def build(g, it1, s):
                ce = bass.ds(g * B, B)
                link(cp(lowg[:, :], lowf[:, ce]))
                tt(hotL[s], lowf[:, ce].unsqueeze(2).to_broadcast([P, B, P]), colf[:, :].unsqueeze(1).to_broadcast([P, B, P]), ALU.is_equal)
                tt(hotH[s], highf[:, ce].unsqueeze(2).to_broadcast([P, B, NB]), colf[:, 0:NB].unsqueeze(1).to_broadcast([P, B, NB]), ALU.is_equal)
                dve.wait_ge(low_landed[s], it1 * 16 + 16)
                ts(hotT[s], dstf[:, s, :, :], nodef[:, 0:1], ALU.is_equal)
                for j in range(B):
                    m = stt(same[s][:, j, :], dstf[:, s, j, :], lowg[:, j:j + 1], tmpm, ALU.is_equal, ALU.mult)
                m.then_inc(built, 1)
                dve.wait_ge(built, g + 3)

            def place_turn(it, last=False):
                for s in range(2):
                    g = it * 2 + s
                    ce = bass.ds(g * B, B)
                    dve.wait_ge(prefix_done, g + 1)
                    link(cp(cell[:, 0, :], cell[:, B, :]))
                    for k in range(2):
                        m = tt(cell[:, 1 + 7 * k:8 + 7 * k, :], psM[:, k, 0:7 * NB].rearrange("p (b w) -> p b w", w=NB),
                               cell[:, 0, :].unsqueeze(1).to_broadcast([P, 7, NB]), ALU.add)
                    m.then_inc(cell_ready, 1)
                    dve.wait_ge(cell_ready, g + 1)
                    if not (last and s):
                        build(g + 1, it + s, 1 - s)
                    dve.wait_ge(place_used, g + 1)
                    for k, values in enumerate((dstF, ew, keyf)):
                        cp(payload[:, s, :, k], values[:, ce])
                    dve.wait_ge(ranks_done, g + 1)
                    for k in range(2):
                        m = tt(picked[:, 7 * k:7 * k + 7, :], psX[:, 512 * k:512 * k + 7 * NB].rearrange("p (b w) -> p b w", b=7),
                               hotH[s][:, 7 * k:7 * k + 7, :], ALU.mult)
                    link(m)
                    link(red(spot[:, :], picked))
                    cp(place[:, s, :], spot[:, :]).then_inc(place_ready, 1)
                    dve.wait_ge(place_ready, g + 1)

            dve.wait_ge(hist_used, 2 * IT + 2)
            link(cp(cell[:, B, :], base))
            build(0, 0, 0)
            with dve.Fori(0, IT - 1) as it:
                st.loop(it, 8)
                place_turn(it)
            st.close(IT - 1)
            place_turn(IT - 1, last=True)

            dve.wait_ge(sorted_in, 16)
            for q in range(2):
                dve.wait_ge(sort_out[q], 16 * B * IT)
            link(dve.memset(src1[:, CH:CH + 2 * B], 0))
            link(dve.tensor_copy(src1[:, 0:CH], sorted3[:, :, 0]))
            link(dve.tensor_copy(ew[:, :], sorted3[:, :, 1]))
            link(dve.memset(cont1[:, 0:1], 0.0))
            link(tt(cont1[:, 1:CH], sorted3[:, 1:CH, 2], sorted3[:, 0:CH - 1, 2], ALU.is_equal))
            link(dve.tensor_copy(cslast[:, 0:1], sorted3[:, 0, 2:3]))
            link(dve.tensor_copy(cslast[:, 1:2], sorted3[:, CH - 1, 2:3]))
            dve.tensor_copy(fixi[:, 2:3], cslast[:, 0:1]).then_inc(firstsrc_ready, 1)
            link(ts(tA, ident[:, :], cslast[:, 0:1], ALU.mult))
            dve.tensor_scalar(tB, ident[:, :], cslast[:, 1:2], None, ALU.mult).then_inc(diag1_ready, 1)
            dve.tensor_tensor(endf, base, cnt, ALU.add).then_inc(ends1_ready, 1)
            dve.wait_ge(ends1_ready, 1)
            dve.wait_ge(diag1_done, 1)
            chain_masks(1, cslast[:, 0:1], cslast[:, 1:2])
            link(ts(has, cnt, 0.0, ALU.is_gt))
            link(stt(scr, endf, float(-1 - EP), has, ALU.add, ALU.mult))
            link(ts(nidx[:, 2, :], scr, float(EP), ALU.add))
            dve.wait_ge(first1_end, 16)
            link(tt(chunkf[:, 1:2], fixr[:, 0:1], chunkf[:, 0:1], ALU.min))
            dve.tensor_scalar(fixi[:, 2:3], chunkf[:, 1:2], -1.0, None, ALU.add).then_inc(order_ready, 1)
            dve.wait_ge(order_ready, 1)

            aq = Steps(n_act)
            ad = Steps(n_actd)
            x = Steps(n_x)
            mm = Steps(n_mm)
            ff2 = Steps(n_ff2)
            stg = Steps(n_stage)
            usd = Steps(nrow_used, 1)
            f1 = t1[:, :, 0:D]
            f2 = t2[:, :, 0:D]

            def bcol(name):
                return bias[:, bb(name), :].unsqueeze(1).to_broadcast([P, KB, D])

            def h4(ap, h):
                return ap.rearrange("p b (h d) -> p b h d", h=h)

            def sm(k, h):
                return small[:, k, 0:KB * h].rearrange("p (b h) -> p b h", h=h)

            def ask(ins):
                ins.then_inc(n_act, 1)
                aq.add()
                ad.add()
                dve.wait_ge(n_actd, ad.value())

            def norm(t, tmp, h, o_, last=None):
                n = D // h
                full = [P, KB, h, n]
                link(red(sm(0, h), h4(t, h)))
                link(ts(sm(0, h), sm(0, h), 1.0 / n, ALU.mult))
                link(tt(h4(t, h), h4(t, h), sm(0, h).unsqueeze(3).to_broadcast(full), ALU.subtract))
                link(tt(h4(tmp, h), h4(t, h), h4(t, h), ALU.mult))
                link(red(sm(1, h), h4(tmp, h)))
                ask(ts(sm(1, h), sm(1, h), 1.0 / n, ALU.mult))
                link(dve.reciprocal(sm(1, h), sm(1, h)))
                m = tt(h4(o_, h), h4(t, h), sm(1, h).unsqueeze(3).to_broadcast(full), ALU.mult)
                if last is None:
                    link(m)
                else:
                    tell(m, last)

            nscat = 0
            for ph in range(6):
                if ph < 5:
                    st4 = stage[:, 0:KB * GW[ph]].rearrange("p (b w) -> p b w", b=KB)
                    if ph == 0:
                        link(dve.memset(st4[:, :, 256:257], 1.0))
                    elif ph == 2:
                        link(dve.memset(h4(st4[:, :, D:GW[2]], 8)[:, :, :, 16:17], 1.0))
                    else:
                        link(dve.memset(h4(st4[:, :, 0:132], 4)[:, :, :, 32:33], 1.0))
                if ph > 0:
                    R = nrow[:, 0:KB * SW[ph - 1]].rearrange("p (b w) -> p b w", b=KB)
                    H, d1, F = HEADS[ph - 1], HD1[ph - 1], FW[ph - 1]
                with dve.Fori(0, KG) as it:
                    st.loop(it, KD[ph])
                    for q, per in ((aq, NAC[ph]), (ad, NAC[ph]), (x, XS[ph]), (mm, [1, 1, 1, 2, 1, 0][ph]), (ff2, int(ph == 3)), (stg, 1),
                                   (usd, int(ph > 0))):
                        q.loop(it, per)
                    Xg = X[:, grp(it), :]
                    Ag = aux[:, grp(it), 0:D]
                    if ph == 0:
                        tell(cp(f1, Xg), x)
                    else:
                        dve.wait_ge(nrow_in, it * (16 * KB) + (16 * KB + (ph - 1) * 16 * NB))
                    if ph == 1:
                        link(tt(f1, Xg, R[:, :, D:D + 1].to_broadcast([P, KB, D]), ALU.mult))
                        tell(tt(f1, f1, R[:, :, 0:D], ALU.subtract), usd)
                        link(tt(f2, Ag, indeg[:, grp(it)].unsqueeze(2).to_broadcast([P, KB, D]), ALU.mult))
                        link(tt(f1, f1, f2, ALU.add))
                        link(tt(f1, f1, Xg, ALU.add))
                        norm(f1, f2, 1, f1, x)
                        link(cp(Xg, f1))
                    if ph == 2:
                        Rh = h4(R[:, :, 0:F], 4)
                        link(ts(sm(2, 4), Rh[:, :, :, 32], 1e-10, ALU.max))
                        link(dve.reciprocal(sm(2, 4), sm(2, 4)))
                        tell(tt(h4(f1, 4), Rh[:, :, :, 0:32], sm(2, 4).unsqueeze(3).to_broadcast([P, KB, 4, 32]), ALU.mult), usd)
                        norm(f1, f2, 4, f1)
                        link(tt(f1, f1, bcol("scale0"), ALU.mult))
                        link(tt(f1, f1, bcol("offset0"), ALU.add))
                        link(tt(f1, f1, Ag, ALU.add))
                        link(stt(f1, f1, 0.5, Xg, ALU.mult, ALU.add))
                        norm(f1, f2, 1, f1, x)
                        link(cp(Xg, f1))
                    if ph == 3:
                        Rh = h4(R[:, :, 0:F], 8)
                        link(ts(sm(2, 8), Rh[:, :, :, 16], 1e-8, ALU.add))
                        link(dve.reciprocal(sm(2, 8), sm(2, 8)))
                        tell(tt(h4(f1, 8), Rh[:, :, :, 0:16], sm(2, 8).unsqueeze(3).to_broadcast([P, KB, 8, 16]), ALU.mult), x)
                        tell(dve.memset(small[:, 11, 0:1], 0.0), usd)
                        mm.add()
                        dve.wait_ge(n_mm, mm.value())
                        link(tt(f2, mmX, bcol("L2_gnn_bo"), ALU.add))
                        link(tt(f2, f2, Xg, ALU.add))
                        norm(f2, f1, 1, f2)
                        link(tt(f2, f2, bcol("L2_gnn_ln1_g"), ALU.mult))
                        tell(tt(f2, f2, bcol("L2_gnn_ln1_b"), ALU.add), x)
                        ff2.add()
                        dve.wait_ge(n_ff2, ff2.value())
                        link(tt(f1, mmX, bcol("L2_gnn_b2"), ALU.add))
                        link(tt(f1, f1, f2, ALU.add))
                        norm(f1, f2, 1, f1)
                        link(tt(f1, f1, bcol("L2_gnn_ln2_g"), ALU.mult))
                        link(tt(f1, f1, bcol("L2_gnn_ln2_b"), ALU.add))
                        link(tt(f1, f1, Xg, ALU.add))
                        norm(f1, f2, 1, f1, x)
                        link(cp(Xg, f1))
                    if ph in (4, 5):
                        Rh = h4(R[:, :, 0:F], 4)
                        mR = R[:, :, F:F + 4]
                        own = aux[:, grp(it), D:D + 4]
                        e1 = small[:, 4, 0:28].rearrange("p (b h) -> p b h", h=4)
                        e2 = small[:, 4, 28:56].rearrange("p (b h) -> p b h", h=4)
                        link(tt(sm(5, 4), mR, own, ALU.max))
                        link(tt(small[:, 3, 0:28].rearrange("p (b h) -> p b h", h=4), mR, sm(5, 4), ALU.subtract))
                        ask(tt(small[:, 3, 28:56].rearrange("p (b h) -> p b h", h=4), own, sm(5, 4), ALU.subtract))
                        link(tt(sm(6, 4), Rh[:, :, :, 32], e1, ALU.mult))
                        link(tt(sm(6, 4), sm(6, 4), e2, ALU.add))
                        link(dve.reciprocal(sm(6, 4), sm(6, 4)))
                        tell(tt(h4(f1, 4), Rh[:, :, :, 0:32], e1.unsqueeze(3).to_broadcast([P, KB, 4, 32]), ALU.mult), usd)
                        link(tt(h4(f2, 4), h4(Ag, 4), e2.unsqueeze(3).to_broadcast([P, KB, 4, 32]), ALU.mult))
                        link(tt(f1, f1, f2, ALU.add))
                        link(tt(h4(f1, 4), h4(f1, 4), sm(6, 4).unsqueeze(3).to_broadcast([P, KB, 4, 32]), ALU.mult))
                        link(tt(f1, f1, bcol("L3_gnn_b1" if ph == 4 else "L3_gnn_b2"), ALU.add))
                        if ph == 4:
                            tell(ts(f1, f1, 0.0, ALU.max), x)
                        else:
                            link(ts(f1, f1, 0.0, ALU.max))
                            link(tt(f1, f1, Xg, ALU.add))
                            norm(f1, f2, 1, Xg, stg)
                    if ph < 5:
                        mm.add()
                        dve.wait_ge(n_mm, mm.value())
                        dve.wait_ge(tab_saved, it * 16 + (16 + 16 * KG * ph))
                        if ZW[ph]:
                            dve.wait_ge(dtab_saved, it * 16 + (16 + 16 * KG * nscat))
                            dve.wait_ge(group_over, it + (1 + KG * ph))
                            z3 = zst[:, 0:KB * ZW[ph]].rearrange("p (b w) -> p b w", b=KB)
                        m1 = mm256[:, :, 0:D]
                        m2 = mm256[:, :, D:2 * D]
                    if ph == 0:
                        link(cp(st4[:, :, 0:D], m1))
                        link(cp(st4[:, :, D:2 * D], Xg))
                        link(tt(Ag, m2, bcol("L0_gnn_b4"), ALU.add))
                        tell(tt(z3, m1, bcol("L0_gnn_b1"), ALU.add), stg)
                    if ph == 1:
                        sv = h4(st4[:, :, 0:132], 4)[:, :, :, 0:32]
                        link(tt(f2, m2, bcol("L1_gnn_b1"), ALU.add))
                        link(ts(sv, h4(f2, 4), 0.0, ALU.max))
                        link(tt(h4(f2, 4), sv, h4(bcol("att"), 4), ALU.mult))
                        link(red(sm(2, 4), h4(f2, 4)))
                        link(stt(st4[:, :, 132:136], sm(2, 4), 0.2, sm(2, 4), ALU.mult, ALU.max))
                        link(tt(f1, m1, bcol("L1_gnn_b0"), ALU.add))
                        link(ts(f1, f1, 0.0, ALU.max))
                        norm(f1, f2, 4, f1)
                        link(tt(f1, f1, bcol("scale1"), ALU.mult))
                        tell(tt(Ag, f1, bcol("offset1"), ALU.add), stg)
                    if ph == 2:
                        link(tt(st4[:, :, 0:D], m1, bcol("L2_gnn_bq"), ALU.add))
                        link(tt(h4(st4[:, :, D:GW[2]], 8)[:, :, :, 0:16], h4(mmX, 8), h4(bcol("L2_gnn_bv"), 8), ALU.add))
                        tell(tt(z3, m2, bcol("L2_gnn_bk"), ALU.add), stg)
                    if ph in (3, 4):
                        link(cp(h4(st4[:, :, 0:132], 4)[:, :, :, 0:32], h4(m1, 4)))
                        link(cp(Ag, m1))
                        link(cp(st4[:, :, 132:136], mm256[:, :, D:D + 4]))
                        link(cp(z3, mm256[:, :, D + 4:D + 8]))
                        link(tt(sm(2, 4), st4[:, :, 132:136], z3, ALU.add))
                        tell(stt(aux[:, grp(it), D:D + 4], sm(2, 4), 0.2, sm(2, 4), ALU.mult, ALU.max), stg)
                for q in (st, aq, ad, x, mm, ff2, stg, usd):
                    q.close(KG)
                if ph == 5:
                    continue
                if ZW[ph]:
                    nscat += 1

                H, d1, F, W, V = HEADS[ph], HD1[ph], FW[ph], SW[ph], VO[ph]
                n = H * (B + 1)

                def hb(ap):
                    return ap[:, 0:n].rearrange("p (h b) -> p h b", h=H)

                if ZW[ph] == 4:
                    dve.wait_ge(slim_in, 16 * (ph - 2))
                    z = rows[:, 0:CH * 4].rearrange("p (c h) -> p c h", h=4)
                    for h in range(4):
                        m = dve.tensor_tensor_scan(ebuf[:, h * CH:(h + 1) * CH], cont[:, :], z[:, :, h], 0.0, ALU.mult, ALU.add)
                        if h < 3:
                            link(m)
                    m.then_inc(slim_done, 1)
                    dve.wait_ge(slim_done, ph - 2)
                e3 = ebuf[:, :].rearrange("p (h c) -> p h c", c=CH)
                for s in range(2):
                    dve.wait_ge(sums_saved[s], 16 + 16 * IT * ph)
                link(dve.memset(sums[:, (2 * B - 1) * W:2 * B * W], 0.0))
                link(dve.memset(dstf[:, 1, B - 1, :], 0.0)) if ZW[ph] == D else None
                link(dve.memset(mx[:, :], 0.0))
                kept = Steps(ebias_kept, 1)
                du = Steps(dst_used, 1 + NG * [0, 0, 1, 0, 0][ph])
                su = Steps(sums_ready, NG * ph)
                ru = Steps(rows_used, 2 + NG * ph)
                sr = Steps(scores_ready, NG * ph)
                holds = Steps(hold_step, (B - 1) * NG * [0, 0, 1, 0, 0][ph])
                accs = Steps(acc_step, (B - 1) * NG * ph)
                parts = Steps(msg_ready)
                wide = int(ZW[ph] == D)

                def expect(g, s):
                    link(cp(cg[:, s, :], (cont1 if ph == 1 else cont)[:, bass.ds(g * B, B)]))
                    if ph:
                        link(ts(hb(nf)[:, :, 1:B + 1], cg[:, s, :].unsqueeze(1).to_broadcast([P, H, B]), -1.0, ALU.add, BIG, ALU.mult))

                def hold(s, j):
                    prev = dstf[:, s, j - 1, :] if j else dstf[:, 1 - s, B - 1, :]
                    if j:
                        dve.wait_ge(hold_step, holds.value())
                    m = stt(dstf[:, s, j, :], prev, cg[:, s, j:j + 1], dstf[:, s, j, :], ALU.mult, ALU.add)
                    if j < B - 1:
                        m.then_inc(hold_step, 1)
                        holds.add()
                    else:
                        m.then_inc(dst_used, 1)
                        du.add()

                def turn(it, last):
                    for s in range(2):
                        g = it * 2 + s
                        ahead = not (last and s)
                        G3 = rows[:, s * B * GW[ph]:(s + 1) * B * GW[ph]].rearrange("p (b w) -> p b w", b=B)
                        S3 = sums[:, s * B * W:(s + 1) * B * W].rearrange("p (b w) -> p b w", b=B)
                        Sp = sums[:, ((2 - s) * B - 1) * W:(2 - s) * B * W]
                        ce = bass.ds(g * B, B)
                        if ph == 1:
                            dve.wait_ge(ebias_done, g + 2)
                            tell(tt(e3[:, :, ce], psX[:, 0:8 * B].rearrange("p (b h) -> p h b", h=8),
                                    beb[:, :].unsqueeze(2).to_broadcast([P, 8, B]), ALU.add), kept)
                        dve.wait_ge(rows_landed[s], it * (16 * B) + (16 * B + ph * IT * 16 * B))
                        if ph == 0:
                            G1 = G3[:, :, 0:D]
                            link(tt(G1, dstf[:, s, :, :], G1, ALU.subtract))
                            link(stt(G1, G1, 0.0, bias[:, bb("L0_gnn_W2"), :].unsqueeze(1).to_broadcast([P, B, D]), ALU.max, ALU.mult))
                            tell(red(ex[:, s * B:(s + 1) * B], G1), sr)
                            if ahead:
                                expect(g + 1, 1 - s)
                            dve.wait_ge(gate_ready, g + 1)
                            link(ts(wt[:, s, :], ex[:, s * B:(s + 1) * B], 1.0, ALU.add))
                            tell(dve.reciprocal(wt[:, s, :], wt[:, s, :]), wr)
                            dve.wait_ge(sums_saved[s], it * 16 + 16)
                        else:
                            link(cp(hb(sc)[:, :, 0], hb(mx)[:, :, B]))
                            s3 = hb(sc)[:, :, 1:B + 1]
                            if ph == 1:
                                link(cp(s3, G3[:, :, 132:136].rearrange("p b h -> p h b")))
                            if ph == 2:
                                link(tt(G3[:, :, 0:D], G3[:, :, 0:D], dstf[:, s, :, :], ALU.mult))
                                link(red(s3.rearrange("p h b -> p b h"), h4(G3[:, :, 0:D], 8)))
                                link(stt(s3, s3, 0.25, e3[:, :, ce], ALU.mult, ALU.add))
                            if ph >= 3:
                                link(tt(s3, G3[:, :, 132:136].rearrange("p b h -> p h b"), e3[:, 0:4, ce], ALU.add))
                                link(stt(s3, s3, 0.2, s3, ALU.mult, ALU.max))
                            link(dve.tensor_tensor_scan(fm[:, 0:n], nf[:, 0:n], sc[:, 0:n], 0.0, ALU.add, ALU.max))
                            link(dve.tensor_tensor_scan(mx[:, 0:n][:, ::-1], nf[:, 1:n + 1][:, ::-1], fm[:, 0:n][:, ::-1], 0.0, ALU.add, ALU.max))
                            tell(tt(df[:, 0:n], sc[:, 0:n], mx[:, 0:n], ALU.subtract), sr)
                            if ahead:
                                expect(g + 1, 1 - s)
                            dve.wait_ge(sums_saved[s], it * 16 + (16 + 16 * IT * ph))
                            link(cp(S3[:, :, F:F + H].rearrange("p b h -> p h b"), hb(mx)[:, :, 1:B + 1]))
                            dve.wait_ge(weights_ready, g + (1 + NG * ph))
                            e3x = hb(ex)[:, :, 1:B + 1]
                            if ph == 1:
                                link(tt(e3x, e3x, ew[:, ce].unsqueeze(1).to_broadcast([P, H, B]), ALU.mult))
                            tell(tt(msg[:, 0:B * F].rearrange("p (b h d) -> p b h d", b=B, h=H), h4(G3[:, :, V:V + F], H),
                                    e3x.rearrange("p h b -> p b h").unsqueeze(3).to_broadcast([P, B, H, d1]), ALU.mult), ru)
                            link(tt(fixr[:, 0:F].rearrange("p (h d) -> p h d", h=H), Sp[:, 0:F].rearrange("p (h d) -> p h d", h=H),
                                    hb(ex)[:, :, 0].unsqueeze(2).to_broadcast([P, H, d1]), ALU.mult))
                        if wide and ahead:
                            nxt = (it + s) * 16 + (16 + 16 * IT * [0, 0, 1][ph])
                            dve.wait_ge(dst_landed[1 - s], nxt)
                        for j in range(B):
                            if ph == 0 and j in [0] + [k + 1 for k in MSG_PARTS[:-1]]:
                                if j <= MSG_PARTS[-2]:
                                    parts.add()
                                    dve.wait_ge(msg_ready, parts.value())
                                else:
                                    dve.wait_ge(rows_used, g + 3)
                            if j:
                                dve.wait_ge(acc_step, accs.value())
                                prev = S3[:, j - 1, 0:F]
                            else:
                                prev = fixr[:, 0:F] if ph else Sp[:, 0:F]
                            m = stt(S3[:, j, 0:F], prev, cg[:, s, j:j + 1], msg[:, j * F:(j + 1) * F], ALU.mult, ALU.add)
                            if j < B - 1:
                                m.then_inc(acc_step, 1)
                                accs.add()
                            else:
                                m.then_inc(sums_ready, 1)
                                su.add()
                            if wide and ahead:
                                hold(1 - s, j)
                        dve.wait_ge(sums_ready, su.value())
                        if wide and ahead:
                            dve.wait_ge(dst_used, du.value())

                wr = Steps(weights_ready)
                expect(0, 0)
                if wide:
                    dve.wait_ge(dst_landed[0], 16 + 16 * IT * [0, 0, 1][ph])
                    for j in range(B):
                        hold(0, j)
                    dve.wait_ge(dst_used, du.value())
                counts = ((st, KE[ph]), (kept, 2 * int(ph == 1)), (du, 2 * wide), (su, 2), (ru, 2 * int(ph > 0)), (sr, 2),
                          (wr, 2 * int(ph == 0)), (holds, 2 * (B - 1) * wide), (accs, 2 * (B - 1)), (parts, 6 * int(ph == 0)))
                with dve.Fori(0, IT - 1) as it:
                    for q, per in counts:
                        q.loop(it, per)
                    turn(it, False)
                for q, _ in counts:
                    q.close(IT - 1)
                turn(IT - 1, True)

                last = sums[:, (2 * B - 1) * W:2 * B * W]
                if ph == 0:
                    dve.wait_ge(st_carry, 1)
                    dve.wait_ge(fix_in, 16)
                    dve.tensor_tensor(fixr[:, 0:F], fixr[:, 0:F], psX[:, 0:F], ALU.add).then_inc(fix_ready, 1)
                    dve.wait_ge(fix_ready, 1)
                    continue
                three = [P, H, P]
                dg = dflat[:, 0:H * P].rearrange("p (h c) -> p h c", h=H)
                vv = dflat[:, 1024:1024 + H * P].rearrange("p (h c) -> p h c", h=H)
                dve.tensor_tensor(dg, ident[:, :].unsqueeze(1).to_broadcast(three), last[:, F:F + H].unsqueeze(2).to_broadcast(three),
                                  ALU.mult).then_inc(st_diag, 1)
                dve.wait_ge(st_max, ph)
                link(tt(vv, psMf[:, 0:H * P].rearrange("p (h c) -> p h c", h=H), fars[int(ph == 1)][:, :].unsqueeze(1).to_broadcast(three), ALU.add))
                link(red(fixk[:, 0:H], vv, ALU.max))
                dve.tensor_tensor(vv, vv, fixk[:, 0:H].unsqueeze(2).to_broadcast(three), ALU.subtract).then_inc(st_diff, 1)
                dve.wait_ge(fix_in, 16 * (ph + 1))
                link(tt(fixk[:, 8:8 + H], fixk[:, 0:H], fixr[:, F:F + H], ALU.max))
                link(tt(fixm[:, 0, 0:H], fixr[:, F:F + H], fixk[:, 8:8 + H], ALU.subtract))
                dve.tensor_tensor(fixm[:, 1, 0:H], fixk[:, 0:H], fixk[:, 8:8 + H], ALU.subtract).then_inc(fix_pair, 1)
                dve.wait_ge(fix_exp, ph)
                dve.wait_ge(st_carry, ph + 1)

                def hd(ap):
                    return ap.rearrange("p (h d) -> p h d", h=H)

                link(tt(hd(msg[:, 0:F]), hd(psX[:, 0:F]), fixm[:, 3, 0:H].unsqueeze(2).to_broadcast([P, H, d1]), ALU.mult))
                link(tt(hd(fixr[:, 0:F]), hd(fixr[:, 0:F]), fixm[:, 2, 0:H].unsqueeze(2).to_broadcast([P, H, d1]), ALU.mult))
                link(tt(fixr[:, 0:F], fixr[:, 0:F], msg[:, 0:F], ALU.add))
                dve.tensor_copy(fixr[:, F:F + H], fixk[:, 8:8 + H]).then_inc(fix_ready, 1)
                dve.wait_ge(fix_ready, ph + 1)


_IN = ["x", "src", "dst", "edge_attr_32", "edge_weight", "L0_gnn_W1", "L0_gnn_b1", "L0_gnn_W2", "L0_gnn_b2",
       "L0_gnn_W4", "L0_gnn_b4", "L1_gnn_W0", "L1_gnn_b0", "L1_gnn_W1", "L1_gnn_b1", "L2_gnn_Wq", "L2_gnn_bq",
       "L2_gnn_Wk", "L2_gnn_bk", "L2_gnn_Wv", "L2_gnn_bv", "L2_gnn_We", "L2_gnn_be", "L2_gnn_Wo", "L2_gnn_bo",
       "L2_gnn_ln1_g", "L2_gnn_ln1_b", "L2_gnn_W1", "L2_gnn_b1", "L2_gnn_W2", "L2_gnn_b2", "L2_gnn_ln2_g",
       "L2_gnn_ln2_b", "L3_gnn_W1", "L3_gnn_a_src1", "L3_gnn_a_dst1", "L3_gnn_b1", "L3_gnn_W2", "L3_gnn_a_src2",
       "L3_gnn_a_dst2", "L3_gnn_b2"]


def kernel(**inputs):
    import numpy as _np
    import concourse.bacc as _bacc
    from concourse import mybir as _mybir
    from concourse.bass_utils import run_bass_kernel_spmd as _run

    named = {n: _np.asarray(inputs[n]) for n in _IN}
    for n in ("L1_gnn_W0", "L1_gnn_W1"):
        named[n] = named[n].T
    for n in ("L0_gnn_W2", "L3_gnn_a_src1", "L3_gnn_a_dst1", "L3_gnn_a_src2", "L3_gnn_a_dst2"):
        named[n] = named[n].reshape(-1)
    named["L2_gnn_b1"] = named["L2_gnn_b1"].reshape(4, 128).T
    attention, scale, offset = (_np.asarray(inputs["L1_gnn_" + n]) for n in ("attention", "scale", "offset"))
    named["att"] = attention[1].reshape(-1)
    for k in range(2):
        named[f"scale{k}"] = scale[k].reshape(-1)
        named[f"offset{k}"] = offset[k].reshape(-1)

    nc = _bacc.Bacc("TRN2", target_bir_lowering=False, num_devices=1)
    arrays, args = {}, {}
    for n, v in named.items():
        v = _np.ascontiguousarray(v)
        arrays[f"in_{n}"] = v
        args[n] = nc.dram_tensor(f"in_{n}", v.shape, _mybir.dt.from_np(v.dtype), kind="ExternalInput").ap()
    out = nc.dram_tensor("out_x", (6250, 128), _mybir.dt.float32, kind="ExternalOutput").ap()
    build(nc, args, out)
    return _run(nc, [arrays], core_ids=[0]).results[0]["out_x"]
```

```python
import concourse.bass as bass
from concourse import mybir
from contextlib import ExitStack

F32 = mybir.dt.float32
I32 = mybir.dt.int32
BF16 = mybir.dt.bfloat16
ALU = mybir.AluOpType
ACT = mybir.ActivationFunctionType
AX = mybir.AxisListType

N = 6250
E = 100000
D = 128
P = 128
CH = 784
EP = P * CH
B = 14
NG = CH // B
IT = NG // 2
NB = 49
NP = NB * P
KB = 7
KG = NB // KB
LASTV = E - (P - 1) * CH
ROWS = N - (NB - 1) * P
BIG = 1e30
BQ = EP // P

HEADS = [1, 4, 8, 4, 4]
HD1 = [129, 33, 17, 33, 33]
FW = [h * d for h, d in zip(HEADS, HD1)]
GW = [257, 136, 264, 136, 136]
VO = [128, 0, 128, 0, 0]
SW = [129, 136, 144, 136, 136]
ZW = [128, 0, 128, 4, 4]
GMAX, SMAX = max(GW), max(SW)

BIAS = ["L0_gnn_b1", "L0_gnn_W2", "L0_gnn_b4", "L1_gnn_b0", "L1_gnn_b1", "att", "scale0", "scale1",
        "offset0", "offset1", "L2_gnn_bq", "L2_gnn_bk", "L2_gnn_bv", "L2_gnn_bo", "L2_gnn_ln1_g",
        "L2_gnn_ln1_b", "L2_gnn_b2", "L2_gnn_ln2_g", "L2_gnn_ln2_b", "L3_gnn_b1", "L3_gnn_b2",
        "L3_gnn_a_src1", "L3_gnn_a_dst1", "L3_gnn_a_src2", "L3_gnn_a_dst2"]


class Steps:

    def __init__(self, sem, start=0):
        self.sem, self.base, self.k, self.it, self.per = sem, start, 0, None, 0

    def loop(self, it, per):
        self.it, self.per, self.k = it, per, 0

    def close(self, turns):
        assert self.k == self.per, (str(self.sem), self.k, self.per)
        self.base += turns * self.per
        self.it, self.k = None, 0

    def add(self, by=1):
        if self.it is None:
            self.base += by
        else:
            self.k += by

    def value(self):
        return self.base if self.it is None else self.it * self.per + (self.base + self.k)


def build(nc, a, out):
    with ExitStack() as ctx:
        def sb(name, shape, dt=F32):
            return ctx.enter_context(nc.sbuf_tensor(name, shape, dt))

        def sem(name):
            return ctx.enter_context(nc.semaphore(name))

        def dram(name, shape, dt=F32):
            return nc.dram_tensor(name, shape, dt, kind="Internal").ap()

        table = [dram(f"table{p}", [NP, GW[p]]) for p in range(5)]
        dst_table = {p: dram(f"dst_table{p}", [NP, ZW[p]]) for p in (0, 2, 3, 4)}
        spread_wide = dram("spread_wide", [EP, D])
        spread_slim = dram("spread_slim", [EP, 4])
        spread = {0: spread_wide, 2: spread_wide, 3: spread_slim, 4: spread_slim}
        states_by_width = {w: dram(f"states{w}", [EP + 1, w]) for w in sorted(set(SW))}
        states = [states_by_width[w] for w in SW]
        attr_tail = dram("attr_tail", [CH, 32])
        dst_rows = dram("dst_rows", [BQ, P])
        samples = dram("samples", [BQ])
        ends = dram("ends", [NP + 1, 1])
        ends_src = dram("ends_src", [NP, 1])
        low_rows = dram("low_rows", [CH, P])
        by_src = dram("by_src", [EP, 3])

        rows = sb("rows", [P, 2 * B * GMAX])
        dstf = sb("dstf", [P, 2, B, D])
        sums = sb("sums", [P, 2 * B * SMAX])
        msg = sb("msg", [P, B * max(FW)])
        ebuf = sb("ebuf", [P, 8 * CH])
        X = sb("X", [P, NB, D])
        aux = sb("aux", [P, NB, 136])
        src = sb("src", [P, CH + 2 * B], I32)
        cont = sb("cont", [P, CH])
        src1 = sb("src1", [P, CH + 2 * B], I32)
        cont1 = sb("cont1", [P, CH])
        colf = sb("colf", [P, P])
        payload = sb("payload", [P, 2, B, 3])
        place = sb("place", [P, 2, B], I32)
        lowg = sb("lowg", [P, B])
        spot = sb("spot", [P, B])
        ew = sb("ew", [P, CH])
        bias = sb("bias", [P, len(BIAS), D])
        ident = sb("ident", [P, P])
        ones = sb("ones", [P, P])
        chains = [sb(f"chain{k}", [P, P]) for k in range(2)]
        fars = [sb(f"far{k}", [P, P]) for k in range(2)]
        WA = [sb(f"WA{p}", [P, 256 if p < 3 else 136]) for p in range(5)]
        Wv = sb("Wv", [P, D])
        Wo = sb("Wo", [P, D])
        W1 = sb("W1", [P, 4 * D])
        W2 = sb("W2", [P, 4, D])
        Web = sb("Web", [P, 32])
        beb = sb("beb", [P, 8])
        b2b = sb("b2b", [P, 1])
        b1c = sb("b1c", [P, 4])
        eps = sb("eps", [P, 2])
        attr = sb("attr", [P, 2, B * 32])
        attrT = sb("attrT", [P, 512])
        idx = sb("idx", [P, 2, B], I32)
        cg = sb("cg", [P, 2, B])
        nf = sb("nf", [P, 8 * (B + 1) + 1])
        sc = sb("sc", [P, 8 * (B + 1)])
        fm = sb("fm", [P, 8 * (B + 1)])
        mx = sb("mx", [P, 8 * (B + 1)])
        df = sb("df", [P, 8 * (B + 1)])
        ex = sb("ex", [P, 8 * (B + 1)])
        wt = sb("wt", [P, 2, B])
        nidx = sb("nidx", [P, 3, NB + KB], I32)
        last_idx = sb("last_idx", [P, KB], I32)
        first_idx = sb("first_idx", [P, KB], I32)
        indeg = sb("indeg", [P, NB])
        small = sb("small", [P, 12, 56])
        fixi = sb("fixi", [P, 4], I32)
        fixr = sb("fixr", [P, SMAX])
        fixm = sb("fixm", [P, 4, 8])
        fixk = sb("fixk", [P, 16])
        zrow = sb("zrow", [P, D])

        stage = rows[:, 0:KB * GMAX]
        nrow = rows[:, KB * GMAX:KB * (GMAX + SMAX)]
        o = KB * (GMAX + SMAX)
        xT = rows[:, o:o + KB * P]
        t1 = rows[:, o + KB * P:o + KB * P + KB * 136].rearrange("p (b d) -> p b d", d=136)
        t2 = rows[:, o + KB * (P + 136):o + KB * (P + 272)].rearrange("p (b d) -> p b d", d=136)
        zst = rows[:, o + KB * (P + 272):o + KB * (2 * P + 272)]
        hT = dstf[:, :, :, :].rearrange("p s b d -> p (s b d)")[:, 0:4 * KB * P].rearrange("p (c n) -> p c n", c=4)
        dflat = dstf[:, :, :, :].rearrange("p s b d -> p (s b d)")
        dsti = ebuf[:, 0:CH].bitcast(I32)
        dstF = ebuf[:, CH:2 * CH]
        junk = ebuf[:, 3 * CH:4 * CH]
        aflat = aux[:, :, :].rearrange("p b d -> p (b d)")
        erow = aflat[:, 0:KB * P].rearrange("p (b d) -> p b d", b=KB)
        at = KB * P
        sampb = aflat[:, at:at + CH]
        scrap = aflat[:, at + CH:at + 2 * CH]
        zeros = aflat[:, at + 2 * CH + 7 * P:at + 2 * CH + 7 * P + B * D]
        tA = junk[:, 0:P]
        tB = junk[:, P:2 * P]
        coli = ebuf[:, 5 * CH:5 * CH + P].bitcast(I32)
        sflat = small[:, :, :].rearrange("p a b -> p (a b)")
        coarse = ebuf[:, 6 * CH:6 * CH + NB]
        fine = ebuf[:, 6 * CH + 64:6 * CH + 64 + NB]
        endf = ebuf[:, 6 * CH + 128:6 * CH + 128 + NB]
        begf = ebuf[:, 6 * CH + 192:6 * CH + 192 + NB]
        nodef = ebuf[:, 6 * CH + 256:6 * CH + 256 + NB]
        nodei = ebuf[:, 6 * CH + 320:6 * CH + 320 + NB].bitcast(I32)
        crsi = ebuf[:, 6 * CH + 384:6 * CH + 384 + NB].bitcast(I32)
        endT = ebuf[0:NB, 7 * CH:7 * CH + P]
        begT = ebuf[0:NB, 7 * CH + P:7 * CH + 2 * P]
        tmpm = ebuf[:, 7 * CH + 2 * P:7 * CH + 3 * P]
        tmp2 = ebuf[:, 7 * CH + 3 * P:7 * CH + 4 * P]
        keyf = ebuf[:, 4 * CH:5 * CH]
        highi = ebuf[:, 5 * CH:6 * CH].bitcast(I32)
        highf = scrap
        highb = junk[:, 0:CH // 2].bitcast(BF16)
        lowb = junk[:, CH // 2:CH].bitcast(BF16)
        numbers = aflat[:, at + 2 * CH + 7 * P + B * D:at + 2 * CH + 7 * P + B * D + B * P // 2].bitcast(BF16).rearrange("p (w b) -> p w b", b=B)
        lowf = ebuf[:, 2 * CH:3 * CH]
        cnt = ebuf[:, 6 * CH + 448:6 * CH + 448 + NB]
        base = ebuf[:, 6 * CH + 512:6 * CH + 512 + NB]
        incl = ebuf[:, 6 * CH + 576:6 * CH + 576 + NB]
        cslast = ebuf[:, 6 * CH + 640:6 * CH + 644]
        LB = CH // 7
        lowT = aflat[0:LB, at + 2 * CH:at + 2 * CH + 7 * P].rearrange("r (b c) -> r b c", b=7)
        ntile = B * P

        def hot(at, w):
            half = B * w // 2
            return rows[:, at:at + half].bitcast(BF16).rearrange("p (b w) -> p b w", b=B)

        def hot_turned(at, w):
            half = B * w // 2
            return rows[:, at:at + half].bitcast(BF16).rearrange("p (w b) -> p w b", b=B)

        hotL = [hot_turned(s * ntile // 2, P) for s in range(2)]
        same = [hot(ntile + s * ntile // 2, P) for s in range(2)]
        hotH = [hot_turned(2 * ntile + s * (B * NB // 2), NB) for s in range(2)]
        hotT = [sums[:, s * ntile:(s + 1) * ntile].rearrange("p (b w) -> p b w", b=B) for s in range(2)]
        cell = msg[:, 0:(B + 1) * NB].rearrange("p (b w) -> p b w", w=NB)
        picked = msg[:, (B + 1) * NB:(2 * B + 1) * NB].rearrange("p (b w) -> p b w", w=NB)
        sorted3 = rows[:, 0:CH * 3].rearrange("p (c k) -> p c k", k=3)
        chunkf = ebuf[:, 7 * CH + 4 * P:7 * CH + 4 * P + 8]

        psT = ctx.enter_context(nc.psum_tensor("psT", [P, 1024], F32))
        psM = ctx.enter_context(nc.psum_tensor("psM", [P, 4, 512], F32))
        psX = ctx.enter_context(nc.psum_tensor("psX", [P, 1024], F32))
        psMf = psM[:, :, :].rearrange("p a b -> p (a b)")
        mm256 = psMf[:, 0:KB * 256].rearrange("p (b d) -> p b d", d=256)
        mmX = psX[:, 0:KB * D].rearrange("p (b d) -> p b d", d=D)

        loaded = sem("loaded")
        attr_ready = sem("attr_ready")
        zeroed = sem("zeroed")
        slim_zeroed = sem("slim_zeroed")
        zero_tile = sem("zero_tile")
        pool_const = sem("pool_const")
        consts = sem("consts")
        dst_saved = sem("dst_saved")
        sampled = sem("sampled")
        samples_in = sem("samples_in")
        search_ready = sem("search_ready")
        search_idx = sem("search_idx")
        search_rows = sem("search_rows")
        search_used = sem("search_used")
        ends_ready = sem("ends_ready")
        endsT_ready = sem("endsT_ready")
        ends_copied = sem("ends_copied")
        ends_saved = sem("ends_saved")
        begs_in = sem("begs_in")
        begs_T = sem("begs_T")
        diag_ready = sem("diag_ready")
        diag_done = sem("diag_done")
        first_ready = sem("first_ready")
        first_end = sem("first_end")
        index_ready = sem("index_ready")
        coarse_done = sem("coarse_done")
        keys_ready = sem("keys_ready")
        lowT_done = sem("lowT_done")
        lowT_copied = sem("lowT_copied")
        low_saved = sem("low_saved")
        hist_ready = sem("hist_ready")
        hist_used = sem("hist_used")
        hist_done = sem("hist_done")
        base_asked = sem("base_asked")
        base_sums = sem("base_sums")
        base_ready = sem("base_ready")
        place_ready = sem("place_ready")
        place_used = sem("place_used")
        sort_out = [sem(f"sort_out{s}") for s in range(2)]
        built = sem("built")
        prefix_done = sem("prefix_done")
        cell_ready = sem("cell_ready")
        ranks_done = sem("ranks_done")
        gate_ready = sem("gate_ready")
        msg_ready = sem("msg_ready")
        hold_step = sem("hold_step")
        acc_step = sem("acc_step")
        sorted_in = sem("sorted_in")
        firstsrc_ready = sem("firstsrc_ready")
        ends1_ready = sem("ends1_ready")
        ends1_T = sem("ends1_T")
        ends1_copied = sem("ends1_copied")
        ends1_saved = sem("ends1_saved")
        first1_end = sem("first1_end")
        diag1_ready = sem("diag1_ready")
        diag1_done = sem("diag1_done")
        order_ready = sem("order_ready")
        low_landed = [sem(f"low_landed{s}") for s in range(2)]
        empty_rows = sem("empty_rows")
        dve_step = sem("dve_step")
        act_step = sem("act_step")
        pool_turn = sem("pool_turn")
        idx_staged = sem("idx_staged")
        rows_landed = [sem(f"rows_landed{s}") for s in range(2)]
        rows_used = sem("rows_used")
        dst_landed = [sem(f"dst_landed{s}") for s in range(2)]
        dst_used = sem("dst_used")
        attr_landed = [sem(f"attr_landed{s}") for s in range(2)]
        attr_turned = sem("attr_turned")
        attr_copied = sem("attr_copied")
        ebias_done = sem("ebias_done")
        ebias_kept = sem("ebias_kept")
        scores_ready = sem("scores_ready")
        weights_ready = sem("weights_ready")
        sums_ready = sem("sums_ready")
        sums_saved = [sem(f"sums_saved{s}") for s in range(2)]
        st_diag = sem("st_diag")
        st_max = sem("st_max")
        st_diff = sem("st_diff")
        st_exp = sem("st_exp")
        st_turn = sem("st_turn")
        st_copy = sem("st_copy")
        st_carry = sem("st_carry")
        fix_in = sem("fix_in")
        fix_pair = sem("fix_pair")
        fix_exp = sem("fix_exp")
        fix_ready = sem("fix_ready")
        fix_out = sem("fix_out")
        last_staged = sem("last_staged")
        first_staged = sem("first_staged")
        nrow_in = sem("nrow_in")
        group_over = sem("group_over")
        nrow_used = sem("nrow_used")
        n_act = sem("n_act")
        n_actd = sem("n_actd")
        n_x = sem("n_x")
        n_t = sem("n_t")
        n_kept = sem("n_kept")
        n_xT = sem("n_xT")
        n_mm = sem("n_mm")
        n_stage = sem("n_stage")
        n_ff = sem("n_ff")
        n_gelu = sem("n_gelu")
        n_ff2 = sem("n_ff2")
        tab_saved = sem("tab_saved")
        dtab_saved = sem("dtab_saved")
        scattered = sem("scattered")
        zfirst_in = sem("zfirst_in")
        zfirst_out = sem("zfirst_out")
        slim_in = sem("slim_in")
        slim_done = sem("slim_done")
        outp = sem("outp")

        def bb(name):
            return BIAS.index(name)

        def grp(it):
            return bass.ds(it * KB, KB)

        LOADS = 8 + len(BIAS) + 3 + 12 + 4
        block = ctx.enter_context(nc.Block())

        XS = [1, 1, 1, 3, 1, 0]
        NAC = [0, 2, 2, 3, 1, 2]
        KD = [3, 23, 19, 32, 14, 16]
        MSG_PARTS = [1, 5, 9, 13]
        KE = [8, 18, 20, 18, 18]

        @block.sync
        def _(sp):
            n = [0]

            def load(dst_ap, src_ap):
                sp.dma_start(dst_ap, src_ap).then_inc(loaded, 16)
                n[0] += 1

            for q, by in ((search_used, 1), (nrow_used, 1), (group_over, 1), (n_stage, 1), (tab_saved, 16), (dtab_saved, 16),
                          (rows_used, 2), (sums_saved[0], 16), (sums_saved[1], 16),
                          (dst_used, 1), (attr_turned, 2), (attr_copied, 1), (ebias_done, 1), (ebias_kept, 1),
                          (hist_used, 2), (built, 2), (place_used, 2)):
                sp.sem_inc(q, by)
            sp.wait_ge(zero_tile, 5)
            load(dsti[0:P - 1, :], a["dst"][0:(P - 1) * CH].rearrange("(p c) -> p c", c=CH))
            load(dsti[P - 1:P, 0:LASTV], a["dst"][(P - 1) * CH:E].rearrange("(p c) -> p c", p=1))
            load(X[:, 0:NB - 1, :], a["x"][0:(NB - 1) * P, :].rearrange("(b p) d -> p b d", p=P))
            load(X[0:ROWS, NB - 1, :], a["x"][(NB - 1) * P:N, :])
            load(src[0:P - 1, 0:CH], a["src"][0:(P - 1) * CH].rearrange("(p c) -> p c", c=CH))
            load(src[P - 1:P, 0:LASTV], a["src"][(P - 1) * CH:E].rearrange("(p c) -> p c", p=1))
            load(ew[0:P - 1, :], a["edge_weight"][0:(P - 1) * CH].rearrange("(p c) -> p c", c=CH))
            load(ew[P - 1:P, 0:LASTV], a["edge_weight"][(P - 1) * CH:E].rearrange("(p c) -> p c", p=1))
            for k, name in enumerate(BIAS):
                load(bias[:, k, :], a[name].rearrange("(o d) -> o d", o=1).to_broadcast([P, D]))
            load(beb[:, :], a["L2_gnn_be"].rearrange("(o d) -> o d", o=1).to_broadcast([P, 8]))
            load(b2b[:, :], a["L0_gnn_b2"].rearrange("(o d) -> o d", o=1).to_broadcast([P, 1]))
            load(b1c[:, :], a["L2_gnn_b1"])
            load(WA[0][:, 0:D], a["L0_gnn_W1"])
            load(WA[0][:, D:2 * D], a["L0_gnn_W4"])
            load(WA[1][:, 0:D], a["L1_gnn_W0"])
            load(WA[1][:, D:2 * D], a["L1_gnn_W1"])
            load(WA[2][:, 0:D], a["L2_gnn_Wq"])
            load(WA[2][:, D:2 * D], a["L2_gnn_Wk"])
            load(WA[3][:, 0:D], a["L3_gnn_W1"])
            load(WA[4][:, 0:D], a["L3_gnn_W2"])
            load(Wv[:, :], a["L2_gnn_Wv"])
            load(Wo[:, :], a["L2_gnn_Wo"])
            load(W1[:, :], a["L2_gnn_W1"])
            load(W2[:, :, :], a["L2_gnn_W2"].rearrange("(c p) n -> p c n", p=P))
            for k in range(4):
                load(Web[32 * k:32 * k + 32, 8 * k:8 * k + 8], a["L2_gnn_We"])
            assert n[0] == LOADS, n[0]

            sp.wait_ge(consts, 1)
            sp.dma_start(states_by_width[129][EP:EP + 1, :], sflat[0:1, 0:129]).then_inc(empty_rows, 16)
            sp.dma_start(states_by_width[144][EP:EP + 1, :], sflat[0:1, 0:144]).then_inc(empty_rows, 16)
            sp.dma_start(states_by_width[136][EP:EP + 1, :], sflat[0:1, 144:280]).then_inc(empty_rows, 16)

            sp.wait_ge(search_ready, 1)
            sp.dma_start(dst_rows.rearrange("r c -> (r c)").rearrange("(p c) -> p c", c=CH), dstF).then_inc(dst_saved, 16)
            sp.wait_ge(dst_saved, 16)
            sp.dma_start(samples.rearrange("(q r) -> q r", q=16),
                         dst_rows[:, 0:1].rearrange("(q r) c -> q (r c)", q=16), allow_slow_non_contiguous=True).then_inc(sampled, 16)
            sp.wait_ge(sampled, 16)
            sp.dma_start(sampb, samples.rearrange("(o r) -> o r", o=1).to_broadcast([P, BQ])).then_inc(samples_in, 16)

            sp.dma_start(spread_slim.rearrange("(p c) d -> p (c d)", c=CH), sums[:, 0:CH * 4]).then_inc(slim_zeroed, 16)
            sp.dma_start(attr_tail[LASTV:CH, :].rearrange("(p r) d -> p (r d)", p=32), zeros[0:32, 0:(CH - LASTV) // 32 * 32]).then_inc(attr_ready, 16)
            sp.dma_start(attr_tail[0:LASTV, :], a["edge_attr_32"][(P - 1) * CH:E, :]).then_inc(attr_ready, 16)

            sp.wait_ge(lowT_copied, 1)
            sp.dma_start(low_rows.rearrange("(b r) c -> r b c", r=LB), lowT).then_inc(low_saved, 16)
            sp.wait_ge(low_saved, 16)
            wide = spread_wide.rearrange("(p c) d -> p c d", c=CH)
            low_all = low_rows.rearrange("r c -> (r c)").rearrange("(o n) -> o n", o=1)
            with sp.Fori(0, IT) as it:
                for s in range(2):
                    g = it * 2 + s
                    sp.wait_ge(built, g + 1)
                    sp.dma_start(dstf[:, s, :, :].rearrange("p b c -> p (b c)"),
                                 low_all[:, bass.ds(g * ntile, ntile)].to_broadcast([P, ntile])).then_inc(low_landed[s], 16)
                    sp.dma_start(wide[:, bass.ds(g * B, B), :].rearrange("p b d -> p (b d)"), zeros).then_inc(zeroed, 16)

            sp.wait_ge(ends_copied, 1)
            sp.dma_start(ends[0:1, :], zrow[0:1, 0:1]).then_inc(ends_saved, 16)
            sp.dma_start(ends[1:NP + 1, :].rearrange("(b p) o -> b (p o)", p=P), endT).then_inc(ends_saved, 16)
            sp.wait_ge(ends_saved, 32)
            sp.dma_start(begT, ends[0:NP, :].rearrange("(b p) o -> b (p o)", p=P)).then_inc(begs_in, 16)
            for s in range(2):
                sp.wait_ge(sort_out[s], 16 * B * IT)
            sp.dma_start(rows[:, 0:CH * 3], by_src.rearrange("(p c) k -> p (c k)", c=CH)).then_inc(sorted_in, 16)
            sp.wait_ge(ends1_copied, 1)
            sp.dma_start(ends_src.rearrange("(b p) o -> b (p o)", p=P), endT).then_inc(ends1_saved, 16)

            tab = Steps(n_stage, 1)
            for ph in range(6):
                if ph < 5:
                    with sp.Fori(0, KG) as it:
                        tab.loop(it, 1)
                        tab.add()
                        sp.wait_ge(n_stage, tab.value())
                        sp.dma_start(table[ph].rearrange("(b p) w -> p b w", p=P)[:, grp(it), :],
                                     stage[:, 0:KB * GW[ph]].rearrange("p (b w) -> p b w", b=KB)).then_inc(tab_saved, 16)
                        if ZW[ph]:
                            sp.dma_start(dst_table[ph].rearrange("(b p) w -> p b w", p=P)[:, grp(it), :],
                                         zst[:, 0:KB * ZW[ph]].rearrange("p (b w) -> p b w", b=KB)).then_inc(dtab_saved, 16)
                    tab.close(KG)
                else:
                    with sp.Fori(0, KG - 1) as it:
                        tab.loop(it, 1)
                        tab.add()
                        sp.wait_ge(n_stage, tab.value())
                        sp.dma_start(out[0:(NB - 1) * P, :].rearrange("(b p) w -> p b w", p=P)[:, grp(it), :],
                                     X[:, grp(it), :]).then_inc(outp, 16)
                    tab.close(KG - 1)
                    tab.add()
                    sp.wait_ge(n_stage, tab.value())
                    sp.dma_start(out[(NB - KB) * P:(NB - 1) * P, :].rearrange("(b p) w -> p b w", p=P),
                                 X[:, NB - KB:NB - 1, :]).then_inc(outp, 16)
                    sp.dma_start(out[(NB - 1) * P:N, :], X[0:ROWS, NB - 1, :]).then_inc(outp, 16)
                    sp.wait_ge(outp, 16 * (KG + 1))
                    continue
                if ZW[ph]:
                    done = [0, 2, 3, 4].index(ph) + 1
                    view = spread[ph].rearrange("(p c) d -> p c d", c=CH)
                    sp.wait_ge(zfirst_in, 16 * done)
                    sp.wait_ge(scattered, 16 * NB * done)
                    sp.dma_start(view[:, 0, :], zrow[:, 0:ZW[ph]]).then_inc(zfirst_out, 16)
                    sp.wait_ge(zfirst_out, 16 * done)
                    if ZW[ph] == 4:
                        sp.wait_ge(tab_saved, 16 + 16 * KG * (ph + 1))
                        sp.wait_ge(dtab_saved, 16 + 16 * KG * done)
                        sp.dma_start(rows[:, 0:CH * 4], view.rearrange("p c d -> p (c d)")).then_inc(slim_in, 16)
                if ZW[ph] == D:
                    q = 1 + [0, 2].index(ph) * NG
                    with sp.Fori(0, IT) as it:
                        for s in range(2):
                            g = it * 2 + s
                            sp.wait_ge(dst_used, g + q)
                            sp.dma_start(dstf[:, s, :, :].rearrange("p b d -> p (b d)"),
                                         view[:, bass.ds(g * B, B), :].rearrange("p b d -> p (b d)")).then_inc(dst_landed[s], 16)
                if ph == 1:
                    sp.wait_ge(attr_ready, 32)
                    with sp.Fori(0, IT) as it:
                        for s in range(2):
                            g = it * 2 + s
                            sp.wait_ge(attr_turned, g + 1)
                            at = bass.ds(g * (B * 32), B * 32)
                            sp.dma_start(attr[0:P - 1, s, :], a["edge_attr_32"][0:(P - 1) * CH, :].rearrange("(p c) d -> p (c d)", c=CH)[:, at]).then_inc(attr_landed[s], 16)
                            sp.dma_start(attr[P - 1:P, s, :], attr_tail.rearrange("(p c) d -> p (c d)", p=1)[:, at]).then_inc(attr_landed[s], 16)

        @block.gpsimd
        def _(pool):
            pool.memset(src[:, :], N).then_inc(zero_tile, 1)
            pool.memset(ew[:, :], 0.0).then_inc(zero_tile, 1)
            pool.memset(dsti, N).then_inc(zero_tile, 1)
            pool.memset(Web[:, :], 0.0).then_inc(zero_tile, 1)
            pool.memset(X[:, NB - 1, :], 0.0).then_inc(zero_tile, 1)
            pool.iota(nodei, pattern=[[P, NB]], base=0, channel_multiplier=1).then_inc(pool_const, 1)
            pool.memset(ident[:, :], 0.0).then_inc(pool_const, 1)
            pool.memset(ones[:, :], 1.0).then_inc(pool_const, 1)
            pool.iota(coli, pattern=[[1, P]], base=0, channel_multiplier=0).then_inc(pool_const, 1)
            pool.iota(fixi[:, 0:2], pattern=[[0, 2]], base=CH, channel_multiplier=CH).then_inc(pool_const, 1)
            pool.wait_ge(pool_const, 5)
            pool.affine_select(out=ident[:, :], in_=ident[:, :], compare_op=ALU.not_equal, fill=1.0, base=0,
                               pattern=[[-1, P]], channel_multiplier=1).then_inc(pool_const, 1)
            pool.affine_select(out=tmpm, in_=ones[:, :], compare_op=ALU.is_gt, fill=0.0, base=0,
                               pattern=[[1, P]], channel_multiplier=-1).then_inc(pool_const, 1)
            pool.affine_select(out=tmp2, in_=ones[:, :], compare_op=ALU.is_gt, fill=0.0, base=0,
                               pattern=[[-1, P]], channel_multiplier=1).then_inc(pool_const, 1)

            turns = Steps(pool_turn)
            with pool.Fori(0, KG) as it:
                pool.wait_ge(search_idx, it + 1)
                pool.sem_inc(pool_turn, 1)
                for b in range(KB):
                    pool.indirect_dma_start(erow[:, b, :], None, dst_rows[:, :],
                                            bass.IndirectOffsetOnAxis(ap=last_idx[:, b:b + 1], axis=0)).then_inc(search_rows, 16)
            def scatter_turn(it, first=False):
                for s in range(2):
                    g = it * 2 + s
                    pool.wait_ge(place_ready, g + 1)
                    pool.sem_inc(pool_turn, 1)
                    for j in range(B):
                        pool.indirect_dma_start(by_src[:, :], bass.IndirectOffsetOnAxis(ap=place[:, s, j:j + 1], axis=0),
                                                payload[:, s, j, :], None).then_inc(sort_out[s], 16)
                    if s or not first:
                        pool.wait_ge(sort_out[1 - s], (it + s) * (16 * B))
                        pool.sem_inc(place_used, 1)

            scatter_turn(0, first=True)
            with pool.Fori(1, IT) as it:
                scatter_turn(it)
            pool.wait_ge(first_ready, 1)
            pool.wait_ge(ends_saved, 32)
            pool.indirect_dma_start(fixr[:, 0:1], None, ends[:, :],
                                    bass.IndirectOffsetOnAxis(ap=fixi[:, 1:2], axis=0)).then_inc(first_end, 16)
            pool.wait_ge(firstsrc_ready, 1)
            pool.wait_ge(ends1_saved, 16)
            pool.wait_ge(index_ready, 1)
            pool.indirect_dma_start(fixr[:, 0:1], None, ends_src[:, :],
                                    bass.IndirectOffsetOnAxis(ap=fixi[:, 2:3], axis=0)).then_inc(first1_end, 16)
            pool.wait_ge(order_ready, 1)
            staged = Steps(n_stage, 1)
            used = Steps(nrow_used, 1)
            nix = Steps(last_staged)
            fix = Steps(first_staged)

            def gather_sums(p):
                nix.add()
                pool.wait_ge(last_staged, nix.value())
                pool.sem_inc(pool_turn, 1)
                pool.wait_ge(nrow_used, used.value())
                pool.sem_inc(pool_turn, 1)
                for b in range(KB):
                    pool.indirect_dma_start(nrow[:, b * SW[p]:(b + 1) * SW[p]], None, states[p][:, :],
                                            bass.IndirectOffsetOnAxis(ap=last_idx[:, b:b + 1], axis=0)).then_inc(nrow_in, 16)
                used.add()

            def spread_rows(ph, g):
                staged.add()
                fix.add()
                pool.wait_ge(first_staged, fix.value())
                pool.sem_inc(pool_turn, 1)
                pool.wait_ge(n_stage, staged.value())
                pool.sem_inc(pool_turn, 1)
                for b in range(KB):
                    pool.indirect_dma_start(spread[ph][:, :], bass.IndirectOffsetOnAxis(ap=first_idx[:, b:b + 1], axis=0),
                                            zst[:, b * ZW[ph]:(b + 1) * ZW[ph]], None,
                                            bounds_check=EP - 1, oob_is_err=False).then_inc(scattered, 16)
                pool.wait_ge(scattered, g * (16 * KB) + (16 * KB + 16 * NB * [0, 2, 3, 4].index(ph)))
                pool.sem_inc(group_over, 1)

            for ph in range(6):
                wide = int(ph in (0, 2, 3, 4))
                if ph == 0:
                    pool.wait_ge(zeroed, 16 * NG)
                    pool.wait_ge(slim_zeroed, 16)
                if ph == 1:
                    pool.wait_ge(empty_rows, 48)
                if ph:
                    gather_sums(ph - 1)
                with pool.Fori(0, KG - 1) as it:
                    staged.loop(it, wide)
                    used.loop(it, int(ph > 0))
                    nix.loop(it, int(ph > 0))
                    fix.loop(it, wide)
                    if ph:
                        gather_sums(ph - 1)
                    if wide:
                        spread_rows(ph, it)
                for q in (staged, used, nix, fix):
                    q.close(KG - 1)
                if wide:
                    spread_rows(ph, KG - 1)
                else:
                    staged.base += KG
                if ph:
                    nix.add()
                if ph == 5:
                    continue
                if ZW[ph]:
                    nz = [0, 2, 3, 4].index(ph)
                    pool.wait_ge(dtab_saved, 16 + 16 * KG * (nz + 1))
                    if nz:
                        pool.wait_ge(zfirst_out, 16 * nz)
                    pool.indirect_dma_start(zrow[:, 0:ZW[ph]], None, dst_table[ph][:, :],
                                            bass.IndirectOffsetOnAxis(ap=fixi[:, 0:1], axis=0)).then_inc(zfirst_in, 16)
                pool.wait_ge(tab_saved, 16 + 16 * KG * (ph + 1))
                if ZW[ph] == 4:
                    pool.wait_ge(slim_done, ph - 2)
                if ZW[ph]:
                    pool.wait_ge(scattered, 16 * NB * (nz + 1))
                with pool.Fori(0, IT) as it:
                    for s in range(2):
                        g = it * 2 + s
                        pool.wait_ge(idx_staged, g + (1 + ph * (NG + 2)))
                        pool.sem_inc(pool_turn, 1)
                        pool.wait_ge(rows_used, g + (1 + ph * NG))
                        pool.sem_inc(pool_turn, 1)
                        for j in range(B):
                            at = (s * B + j) * GW[ph]
                            pool.indirect_dma_start(rows[:, at:at + GW[ph]], None, table[ph][:, :],
                                                    bass.IndirectOffsetOnAxis(ap=idx[:, s, j:j + 1], axis=0)).then_inc(rows_landed[s], 16)
                for s in range(2):
                    pool.wait_ge(sums_saved[s], 16 + 16 * IT * (ph + 1))
                k = 2 if ph == 1 else 1
                pool.indirect_dma_start(fixr[:, 0:SW[ph]], None, states[ph][:, :],
                                        bass.IndirectOffsetOnAxis(ap=fixi[:, k:k + 1], axis=0)).then_inc(fix_in, 16)
                pool.wait_ge(fix_ready, ph + 1)
                pool.indirect_dma_start(states[ph][:, :], bass.IndirectOffsetOnAxis(ap=fixi[:, k:k + 1], axis=0),
                                        fixr[:, 0:SW[ph]], None).then_inc(fix_out, 16)
                pool.wait_ge(fix_out, 16 * (ph + 1))

        @block.tensor
        def _(pe):
            def turn(blocks, src_of):
                for b in range(blocks):
                    last = pe.transpose(psT[:, b * P:(b + 1) * P], src_of(b), ident[:, :])
                return last

            pe.wait_ge(pool_const, 8)
            pe.wait_ge(loaded, 16 * LOADS)
            pe.wait_ge(consts, 1)
            pe.wait_ge(diag_ready, 1)
            pe.matmul(psX[:, 0:P], ones[:, :], tA, start=True, stop=True)
            pe.matmul(psX[:, P:2 * P], ones[:, :], tB, start=True, stop=True).then_inc(diag_done, 1)
            pe.wait_ge(keys_ready, 1)
            for b in range(7):
                m = pe.transpose(psT[0:LB, b * P:(b + 1) * P], lowf[:, b * LB:(b + 1) * LB], ident[:, :])
            m.then_inc(lowT_done, 1)
            cells = psM[:, 0, 0:NB]
            pe.wait_ge(lowT_copied, 1)
            pe.matmul(cells, ident[:, :], zrow[:, 0:NB], start=True, stop=True)
            with pe.Fori(0, IT) as it:
                for s in range(2):
                    g = it * 2 + s
                    pe.wait_ge(hist_ready, g + 1)
                    for j in range(B):
                        m = pe.matmul(cells, hotL[s][:, :, j], hotH[s][:, :, j], start=False, stop=True, skip_group_check=True)
                    m.then_inc(hist_used, 1)
            pe.matmul(cells, ident[:, :], zrow[:, 0:NB], start=False, stop=True, skip_group_check=True).then_inc(hist_done, 1)
            pe.wait_ge(base_asked, 1)
            pe.matmul(psX[:, 0:NB], tmpm, cnt, start=True, stop=True)
            pe.matmul(psX[:, 64:64 + NB], ones[:, :], cnt, start=True, stop=True).then_inc(base_sums, 1)
            pe.wait_ge(base_ready, 1)

            def prefixes(s):
                for i in range(B):
                    for k in range(2):
                        lo = max(i, 7 * k)
                        if lo < 7 * k + 7:
                            m = pe.matmul(psM[:, k, (lo - 7 * k) * NB:7 * NB].rearrange("p (c w) -> p c w", w=NB), hotL[s][:, :, i],
                                          hotH[s][:, :, i].unsqueeze(1).to_broadcast([P, 7 * k + 7 - lo, NB]),
                                          start=(i == 0), stop=(i == 7 * k + 6))
                m.then_inc(prefix_done, 1)

            def rank_turn(it, last=False):
                for s in range(2):
                    g = it * 2 + s
                    pe.wait_ge(cell_ready, g + 1)
                    for j in range(B):
                        t = psX[:, j // 7 * 512 + j % 7 * NB:j // 7 * 512 + (j % 7 + 1) * NB]
                        pe.matmul(t, hotT[s][:, j, :], cell[:, j, :], start=True, stop=False)
                        m = pe.matmul(t, same[s][:, j, :], hotH[s][:, :, j], start=False, stop=True)
                    m.then_inc(ranks_done, 1)
                    if not (last and s):
                        pe.wait_ge(built, g + 4)
                        prefixes(1 - s)

            pe.wait_ge(built, 3)
            prefixes(0)
            with pe.Fori(0, IT - 1) as it:
                rank_turn(it)
            rank_turn(IT - 1, last=True)
            pe.wait_ge(ends_ready, 1)
            pe.transpose(psT[0:NB, 0:P], endf, ident[:, :]).then_inc(endsT_ready, 1)
            pe.wait_ge(begs_in, 16)
            pe.wait_ge(ends_copied, 1)
            pe.transpose(psT[:, 512:512 + NB], begT, ident[0:NB, 0:NB]).then_inc(begs_T, 1)
            pe.wait_ge(index_ready, 1)

            pe.wait_ge(diag1_ready, 1)
            pe.matmul(psX[:, 0:P], ones[:, :], tA, start=True, stop=True)
            pe.matmul(psX[:, P:2 * P], ones[:, :], tB, start=True, stop=True).then_inc(diag1_done, 1)
            pe.wait_ge(ends1_ready, 1)
            pe.transpose(psT[0:NB, 0:P], endf, ident[:, :]).then_inc(ends1_T, 1)
            pe.wait_ge(order_ready, 1)

            x = Steps(n_x)
            xt = Steps(n_xT)
            gel = Steps(n_gelu)
            for ph in range(5):
                with pe.Fori(0, KG) as it:
                    per = XS[ph]
                    x.loop(it, per)
                    xt.loop(it, per)
                    free = it + (1 + KG * ph)
                    gel.loop(it, 8)
                    if ph == 3:
                        x.add()
                        pe.wait_ge(n_x, x.value())
                        turn(KB, lambda b: t1[:, b, 0:D]).then_inc(n_t, 1)
                        xt.add()
                        pe.wait_ge(n_xT, xt.value())
                        for b in range(KB):
                            m = pe.matmul(mmX[:, b, :], xT[:, b * P:(b + 1) * P], Wo[:, :], start=True, stop=True)
                        m.then_inc(n_mm, 1)
                        x.add()
                        pe.wait_ge(n_x, x.value())
                        turn(KB, lambda b: t2[:, b, 0:D]).then_inc(n_t, 1)
                        xt.add()
                        pe.wait_ge(n_xT, xt.value())
                        pe.wait_ge(n_stage, free)
                        for half in range(2):
                            for c in range(2):
                                for q in range(2):
                                    if half:
                                        gel.add()
                                        pe.wait_ge(n_gelu, gel.value())
                                    pe.matmul(psM[:, c * 2 + q, 0:448], W1[:, (half * 2 + c) * P:(half * 2 + c + 1) * P],
                                              xT[:, q * 448:(q + 1) * 448], start=True, stop=True).then_inc(n_ff, 1)
                        gel.add(4)
                        pe.wait_ge(n_gelu, gel.value())
                        for b in range(KB):
                            for c in range(4):
                                m = pe.matmul(mmX[:, b, :], hT[:, c, b * P:(b + 1) * P], W2[:, c, :], start=(c == 0), stop=(c == 3))
                        m.then_inc(n_ff2, 1)
                    x.add()
                    pe.wait_ge(n_x, x.value())
                    turn(KB, lambda b: t1[:, b, 0:D]).then_inc(n_t, 1)
                    xt.add()
                    pe.wait_ge(n_xT, xt.value())
                    w = 256 if ph < 3 else 136
                    pe.wait_ge(n_stage, free)
                    for b in range(KB):
                        m = pe.matmul(mm256[:, b, 0:w], xT[:, b * P:(b + 1) * P], WA[ph][:, :], start=True, stop=True)
                        if ph == 2:
                            m = pe.matmul(mmX[:, b, :], xT[:, b * P:(b + 1) * P], Wv[:, :], start=True, stop=True)
                    m.then_inc(n_mm, 1)
                x.close(KG)
                xt.close(KG)
                if ph == 3:
                    gel.close(KG)
                if ph == 1:
                    with pe.Fori(0, IT) as it:
                        for s in range(2):
                            g = it * 2 + s
                            pe.wait_ge(attr_landed[s], it * 32 + 32)
                            pe.wait_ge(attr_copied, g + 1)
                            for q in range(4):
                                w = P if q < 3 else 64
                                m = pe.transpose(psT[0:w, q * P:(q + 1) * P], attr[:, s, q * P:q * P + w], ident[:, :])
                            m.then_inc(attr_turned, 1)
                            pe.wait_ge(attr_copied, g + 2)
                            pe.wait_ge(ebias_kept, g + 1)
                            for q in range(4):
                                w = P if q < 3 else 64
                                m = pe.matmul(psX[:, q * 32:q * 32 + w // 4], attrT[0:w, q * P:(q + 1) * P], Web[0:w, 0:w // 4],
                                              start=True, stop=True)
                            m.then_inc(ebias_done, 1)
                H, F, d1 = HEADS[ph], FW[ph], HD1[ph]
                last = sums[:, (B + B - 1) * SW[ph]:2 * B * SW[ph]]
                pe.wait_ge(sums_ready, NG * (ph + 1))
                if ph == 0:
                    pe.matmul(psX[:, 0:F], chains[0][:, :], last[:, 0:F], start=True, stop=True).then_inc(st_carry, 1)
                    continue
                pe.wait_ge(st_diag, ph)
                for k in range(H // 4):
                    m = pe.matmul(psM[:, k, :], ones[:, :], dflat[:, k * 512:(k + 1) * 512], start=True, stop=True)
                m.then_inc(st_max, 1)
                pe.wait_ge(st_exp, ph)
                for h in range(H):
                    m = pe.transpose(psM[:, 2 + h // 4, h % 4 * P:(h % 4 + 1) * P], dflat[:, 1024 + h * P:1024 + (h + 1) * P], ident[:, :])
                m.then_inc(st_turn, 1)
                pe.wait_ge(st_copy, ph)
                for h in range(H):
                    m = pe.matmul(psX[:, h * d1:(h + 1) * d1], dflat[:, 2048 + h * P:2048 + (h + 1) * P],
                                  last[:, h * d1:(h + 1) * d1], start=True, stop=True)
                m.then_inc(st_carry, 1)

        @block.scalar
        def _(act):
            step = Steps(act_step)
            act.wait_ge(lowT_done, 1)
            act.activation(lowT[:, 0:4, :].rearrange("r b c -> r (b c)"), psT[0:LB, 0:512], ACT.Copy)
            act.activation(lowT[:, 4:7, :].rearrange("r b c -> r (b c)"), psT[0:LB, 512:7 * P], ACT.Copy).then_inc(lowT_copied, 1)
            used = Steps(search_used, 1)
            act.wait_ge(coarse_done, 1)
            with act.Fori(0, KG) as it:
                used.loop(it, 1)
                act.wait_ge(search_used, used.value())
                act.sem_inc(act_step, 1)
                act.activation(last_idx[:, :], crsi[:, grp(it)], ACT.Copy).then_inc(search_idx, 1)
                used.add()
            used.close(KG)
            act.wait_ge(endsT_ready, 1)
            act.activation(endT, psT[0:NB, 0:P], ACT.Copy).then_inc(ends_copied, 1)
            act.wait_ge(index_ready, 1)
            act.wait_ge(ends1_T, 1)
            act.activation(endT, psT[0:NB, 0:P], ACT.Copy).then_inc(ends1_copied, 1)
            act.wait_ge(order_ready, 1)

            t = Steps(n_t)
            aq = Steps(n_act)
            ff = Steps(n_ff)
            for ph in range(6):
                def turned():
                    t.add()
                    act.wait_ge(n_t, t.value())
                    act.activation(xT[:, 0:512], psT[:, 0:512], ACT.Copy)
                    act.activation(xT[:, 512:KB * P], psT[:, 512:KB * P], ACT.Copy).then_inc(n_xT, 1)

                def call(o_ap, i_ap, f, **kw):
                    aq.add()
                    act.wait_ge(n_act, aq.value())
                    act.activation(o_ap, i_ap, f, **kw).then_inc(n_actd, 1)

                def root(k, n, e):
                    call(small[:, k, 0:n], small[:, k, 0:n], ACT.Sqrt, scale=n / (KB * D), bias=eps[:, e:e + 1])

                def sums_index(g):
                    act.activation(last_idx[:, :], nidx[:, 2 if ph == 2 else 0, grp(g)], ACT.Copy).then_inc(last_staged, 1)

                def features(g):
                    if ph:
                        act.wait_ge(nrow_in, g * (16 * KB) + (16 * KB + 16 * NB * (ph - 1)))
                        act.sem_inc(act_step, 1)
                        sums_index(g + 1)
                    if ph == 1:
                        root(1, KB, 0)
                    if ph == 2:
                        root(1, 28, 1)
                        root(1, KB, 0)
                    if ph == 3:
                        turned()
                        root(1, KB, 0)
                        turned()
                        for half in range(2):
                            for c in range(2):
                                for q in range(2):
                                    ff.add()
                                    act.wait_ge(n_ff, ff.value())
                                    act.activation(hT[:, half * 2 + c, q * 448:(q + 1) * 448], psM[:, c * 2 + q, 0:448], ACT.Gelu,
                                                   scale=1.0, bias=b1c[:, half * 2 + c:half * 2 + c + 1]).then_inc(n_gelu, 1)
                        root(1, KB, 0)
                        root(1, KB, 0)
                        turned()
                    if ph in (4, 5):
                        call(small[:, 4, 0:56], small[:, 3, 0:56], ACT.Exp)
                    if ph == 5:
                        root(1, KB, 0)
                    if ph in (0, 1, 2, 4):
                        turned()
                    if ph in (1, 2, 3):
                        act.activation(X[:, grp(g), :], t1[:, :, 0:D], ACT.Copy).then_inc(n_kept, 1)

                def tables(g, ahead=False):
                    if ph == 1:
                        root(1, 28, 1)
                    if ph in (0, 2, 4) or ph == 3 and ahead:
                        act.wait_ge(group_over, g + (1 + KG * [0, 2, 3, 4].index(ph)))
                        act.sem_inc(act_step, 1)
                        act.activation(first_idx[:, :], nidx[:, 1, grp(g)], ACT.Copy).then_inc(first_staged, 1)

                if ph:
                    sums_index(0)
                features(0)
                with act.Fori(0, KG - 1) as it:
                    t.loop(it, XS[ph])
                    aq.loop(it, NAC[ph])
                    ff.loop(it, 8 * int(ph == 3))
                    if ph == 3:
                        tables(it, ahead=True)
                    features(it + 1)
                    tables(it)
                for q in (t, aq, ff):
                    q.close(KG - 1)
                tables(KG - 1, ahead=True)
                if ph == 5:
                    continue
                H, d1, F, W = HEADS[ph], HD1[ph], FW[ph], SW[ph]
                act.wait_ge(rows_used, 2 + ph * NG)
                source = src1 if ph == 1 else src
                for s in range(2):
                    act.activation(idx[:, s, :], source[:, s * B:(s + 1) * B], ACT.Copy).then_inc(idx_staged, 1)
                with act.Fori(0, IT) as it:
                    for s in range(2):
                        g = it * 2 + s
                        if ph == 1:
                            act.wait_ge(attr_turned, g + 3)
                            act.sem_inc(act_step, 1)
                            act.activation(attrT[:, 0:3 * P], psT[:, 0:3 * P], ACT.Copy)
                            act.activation(attrT[0:64, 3 * P:4 * P], psT[0:64, 3 * P:4 * P], ACT.Copy).then_inc(attr_copied, 1)
                        act.wait_ge(scores_ready, g + (1 + ph * NG))
                        if ph == 0:
                            act.activation(ex[:, s * B:(s + 1) * B], ex[:, s * B:(s + 1) * B], ACT.Exp, scale=-1.0, bias=b2b[:, 0:1]).then_inc(gate_ready, 1)
                            act.wait_ge(weights_ready, g + 1)
                            act.sem_inc(act_step, 1)
                            for j in range(B):
                                at = (s * B + j) * GW[0] + D
                                m = act.activation(msg[:, j * F:(j + 1) * F], rows[:, at:at + F], ACT.Copy, scale=wt[:, s, j:j + 1])
                                if j in MSG_PARTS[:-1]:
                                    m.then_inc(msg_ready, 1)
                            m.then_inc(rows_used, 1)
                        else:
                            n = H * (B + 1)
                            act.activation(ex[:, 0:n], df[:, 0:n], ACT.Exp).then_inc(weights_ready, 1)
                        act.wait_ge(rows_used, g + (3 + ph * NG))
                        act.sem_inc(act_step, 1)
                        act.activation(idx[:, s, :], source[:, bass.ds((g + 2) * B, B)], ACT.Copy).then_inc(idx_staged, 1)
                        act.wait_ge(sums_ready, g + (1 + ph * NG))
                        act.dma_start(states[ph][0:EP, :].rearrange("(p c) w -> p c w", c=CH)[:, bass.ds(g * B, B), :].rearrange("p b w -> p (b w)"),
                                      sums[:, s * B * W:(s + 1) * B * W]).then_inc(sums_saved[s], 16)
                if ph == 0:
                    continue
                act.wait_ge(st_diff, ph)
                act.activation(dflat[:, 1024:1024 + H * P], dflat[:, 1024:1024 + H * P], ACT.Exp).then_inc(st_exp, 1)
                act.wait_ge(st_turn, ph)
                for k in range(H // 4):
                    m = act.activation(dflat[:, 2048 + k * 512:2048 + (k + 1) * 512], psM[:, 2 + k, :], ACT.Copy)
                m.then_inc(st_copy, 1)
                act.wait_ge(fix_pair, ph)
                act.activation(fixm[:, 2:4, 0:H], fixm[:, 0:2, 0:H], ACT.Exp).then_inc(fix_exp, 1)

        @block.vector
        def _(dve):
            st = Steps(dve_step)

            def link(ins):
                ins.then_inc(dve_step, 1)
                st.add()
                dve.wait_ge(dve_step, st.value())

            def note(ins):
                ins.then_inc(dve_step, 1)
                st.add()

            def tell(ins, steps):
                ins.then_inc(steps.sem, 1)
                steps.add()
                dve.wait_ge(steps.sem, steps.value())

            def tt(o_, a_, b_, op):
                return dve.tensor_tensor(o_, a_, b_, op)

            def ts(o_, a_, s1, op0, s2=None, op1=None):
                if op1 is None:
                    return dve.tensor_scalar(o_, a_, s1, None, op0)
                return dve.tensor_scalar(o_, a_, s1, s2, op0, op1)

            def cp(o_, a_):
                return dve.tensor_scalar(o_, a_, 1.0, None, ALU.mult)

            def stt(o_, a_, s_, b_, op0, op1):
                return dve.scalar_tensor_tensor(o_, a_, s_, b_, op0, op1)

            def red(o_, a_, op=ALU.add):
                return dve.tensor_reduce(o_, a_, AX.X, op)

            link(dve.memset(sums[:, :], 0.0))
            link(dve.memset(msg[:, :], 0.0))
            link(dve.memset(zrow[:, :], 0.0))
            link(dve.memset(nidx[:, :, :], 0))
            link(dve.memset(zeros, 0.0))
            link(dve.memset(eps[:, 0:1], 1e-5))
            link(dve.memset(eps[:, 1:2], 1e-9))
            link(dve.memset(nf[:, :], -BIG))
            link(dve.memset(sflat[:, 0:280], 0.0))
            link(dve.memset(sflat[:, 136:144], -BIG))
            dve.memset(sflat[:, 276:280], -BIG).then_inc(consts, 1)
            dve.wait_ge(consts, 1)
            dve.wait_ge(loaded, 16 * LOADS)
            dve.wait_ge(pool_const, 8)
            link(ts(b2b[:, :], b2b[:, :], -1.0, ALU.mult))
            dve.tensor_copy(dstF, dsti).then_inc(search_ready, 1)
            dve.wait_ge(search_ready, 1)
            link(dve.tensor_copy(nodef, nodei))
            link(ts(tA, ident[:, :], dstF[:, 0:1], ALU.mult))
            dve.tensor_scalar(tB, ident[:, :], dstF[:, CH - 1:CH], None, ALU.mult).then_inc(diag_ready, 1)
            link(dve.tensor_copy(chunkf[:, 0:1], fixi[:, 0:1]))
            link(dve.tensor_copy(fixi[:, 0:1], dstF[:, 0:1]))
            dve.tensor_scalar(fixi[:, 1:2], dstF[:, 0:1], 1.0, None, ALU.add).then_inc(first_ready, 1)
            link(dve.memset(cont[:, 0:1], 0.0))
            link(tt(cont[:, 1:CH], dstF[:, 1:CH], dstF[:, 0:CH - 1], ALU.is_equal))
            link(dve.tensor_copy(colf[:, :], coli))

            def chain_masks(k, first, last):
                link(stt(chains[k][:, :], psX[:, 0:P], last, tmpm, ALU.is_equal, ALU.mult))
                link(stt(fars[k][:, :], psX[:, P:2 * P], first, tmp2, ALU.is_equal, ALU.mult))
                link(ts(fars[k][:, :], fars[k][:, :], -1.0, ALU.add, BIG, ALU.mult))

            dve.wait_ge(diag_done, 1)
            chain_masks(0, dstF[:, 0:1], dstF[:, CH - 1:CH])
            for p, (ks, kd) in ((3, ("L3_gnn_a_src1", "L3_gnn_a_dst1")), (4, ("L3_gnn_a_src2", "L3_gnn_a_dst2"))):
                for k, name in enumerate((ks, kd)):
                    link(tt(junk[:, 256:384], WA[p][:, 0:D], bias[:, bb(name), :], ALU.mult))
                    link(red(WA[p][:, D + 4 * k:D + 4 * k + 4], junk[:, 256:384].rearrange("p (h d) -> p h d", h=4)))

            link(ts(highi, src[:, 0:CH], 7, ALU.arith_shift_right))
            link(dve.tensor_copy(highf, highi))
            link(dve.tensor_copy(keyf, src[:, 0:CH]))
            dve.scalar_tensor_tensor(lowf, highf, float(-P), keyf, ALU.mult, ALU.add).then_inc(keys_ready, 1)
            dve.wait_ge(keys_ready, 1)
            link(dve.tensor_copy(highb, highf))
            link(dve.tensor_copy(lowb, lowf))
            link(dve.tensor_copy(numbers, colf[:, :].unsqueeze(2).to_broadcast([P, P, B])))
            dve.wait_ge(samples_in, 16)
            with dve.Fori(0, NB) as b:
                st.loop(b, 1)
                link(dve.tensor_scalar(scrap, sampb, nodef[:, bass.ds(b, 1)], 0.0, ALU.is_le, ALU.add,
                                       accum_out=coarse[:, bass.ds(b, 1)]))
            st.close(NB)
            link(ts(coarse, coarse, -1.0, ALU.add, 0.0, ALU.max))
            dve.tensor_copy(crsi, coarse).then_inc(coarse_done, 1)
            GS = NG // KG
            use = Steps(search_used, 1)
            with dve.Fori(0, KG) as it:
                use.loop(it, 1)
                st.loop(it, KB - 1)
                for k in range(GS):
                    s, g = k % 2, it * GS + k
                    ce = bass.ds(g * B, B)
                    dve.wait_ge(hist_used, g + 1)
                    tt(hotL[s], lowb[:, ce].unsqueeze(1).to_broadcast([P, P, B]), numbers, ALU.is_equal)
                    tt(hotH[s], highb[:, ce].unsqueeze(1).to_broadcast([P, NB, B]), numbers[:, 0:NB, :], ALU.is_equal).then_inc(hist_ready, 1)
                dve.wait_ge(search_rows, it * (16 * KB) + 16 * KB)
                for b in range(KB):
                    m = dve.tensor_scalar(scrap[:, 0:P], erow[:, b, :], nodef[:, bass.ds(it * KB + b, 1)], 0.0, ALU.is_le, ALU.add,
                                          accum_out=fine[:, bass.ds(it * KB + b, 1)])
                    if b < KB - 1:
                        link(m)
                    else:
                        tell(m, use)
            use.close(KG)
            st.close(KG)
            dve.wait_ge(hist_done, 1)
            dve.tensor_copy(cnt, psM[:, 0, 0:NB]).then_inc(base_asked, 1)
            dve.wait_ge(base_asked, 1)
            dve.wait_ge(base_sums, 1)
            link(dve.tensor_tensor_scan(incl, ones[:, 0:NB], psX[:, 64:64 + NB], 0.0, ALU.mult, ALU.add))
            link(tt(incl, incl, psX[:, 64:64 + NB], ALU.subtract))
            dve.tensor_tensor(base, incl, psX[:, 0:NB], ALU.add).then_inc(base_ready, 1)
            dve.wait_ge(base_ready, 1)

            def build(g, it1, s):
                ce = bass.ds(g * B, B)
                link(cp(lowg[:, :], lowf[:, ce]))
                tt(hotL[s], lowb[:, ce].unsqueeze(1).to_broadcast([P, P, B]), numbers, ALU.is_equal)
                tt(hotH[s], highb[:, ce].unsqueeze(1).to_broadcast([P, NB, B]), numbers[:, 0:NB, :], ALU.is_equal)
                dve.wait_ge(low_landed[s], it1 * 16 + 16)
                ts(hotT[s], dstf[:, s, :, :], nodef[:, 0:1], ALU.is_equal)
                for j in range(B):
                    m = stt(same[s][:, j, :], dstf[:, s, j, :], lowg[:, j:j + 1], tmpm, ALU.is_equal, ALU.mult)
                m.then_inc(built, 1)
                dve.wait_ge(built, g + 3)

            def place_turn(it, last=False):
                for s in range(2):
                    g = it * 2 + s
                    ce = bass.ds(g * B, B)
                    dve.wait_ge(prefix_done, g + 1)
                    link(cp(cell[:, 0, :], cell[:, B, :]))
                    for k in range(2):
                        m = tt(cell[:, 1 + 7 * k:8 + 7 * k, :], psM[:, k, 0:7 * NB].rearrange("p (b w) -> p b w", w=NB),
                               cell[:, 0, :].unsqueeze(1).to_broadcast([P, 7, NB]), ALU.add)
                    m.then_inc(cell_ready, 1)
                    dve.wait_ge(cell_ready, g + 1)
                    if not (last and s):
                        build(g + 1, it + s, 1 - s)
                    dve.wait_ge(place_used, g + 1)
                    for k, values in enumerate((dstF, ew, keyf)):
                        cp(payload[:, s, :, k], values[:, ce])
                    dve.wait_ge(ranks_done, g + 1)
                    for k in range(2):
                        m = tt(picked[:, 7 * k:7 * k + 7, :], psX[:, 512 * k:512 * k + 7 * NB].rearrange("p (b w) -> p b w", b=7),
                               hotH[s][:, :, 7 * k:7 * k + 7].rearrange("p w b -> p b w"), ALU.mult)
                    link(m)
                    link(red(spot[:, :], picked))
                    cp(place[:, s, :], spot[:, :]).then_inc(place_ready, 1)
                    dve.wait_ge(place_ready, g + 1)

            dve.wait_ge(hist_used, 2 * IT + 2)
            dve.wait_ge(slim_zeroed, 16)
            link(cp(cell[:, B, :], base))
            build(0, 0, 0)
            with dve.Fori(0, IT - 1) as it:
                st.loop(it, 8)
                place_turn(it)
            st.close(IT - 1)
            place_turn(IT - 1, last=True)

            dve.scalar_tensor_tensor(endf, coarse, float(P), fine, ALU.mult, ALU.add).then_inc(ends_ready, 1)
            dve.wait_ge(ends_ready, 1)
            dve.wait_ge(begs_T, 1)
            link(dve.tensor_copy(begf, psT[:, 512:512 + NB]))
            link(tt(indeg[:, :], endf, begf, ALU.subtract))
            has = scrap[:, 0:NB]
            scr = scrap[:, 64:64 + NB]
            link(ts(has, indeg[:, :], 0.0, ALU.is_gt))
            link(stt(scr, endf, float(-1 - EP), has, ALU.add, ALU.mult))
            link(ts(nidx[:, 0, 0:NB], scr, float(EP), ALU.add))
            link(ts(has, has, float(-EP), ALU.mult, float(EP), ALU.add))
            link(tt(nidx[:, 1, 0:NB], has, begf, ALU.add))
            dve.wait_ge(first_end, 16)
            link(tt(chunkf[:, 1:2], fixr[:, 0:1], chunkf[:, 0:1], ALU.min))
            dve.tensor_scalar(fixi[:, 1:2], chunkf[:, 1:2], -1.0, None, ALU.add).then_inc(index_ready, 1)
            dve.wait_ge(index_ready, 1)

            dve.wait_ge(sorted_in, 16)
            for q in range(2):
                dve.wait_ge(sort_out[q], 16 * B * IT)
            link(dve.memset(src1[:, CH:CH + 2 * B], 0))
            link(dve.tensor_copy(src1[:, 0:CH], sorted3[:, :, 0]))
            link(dve.tensor_copy(ew[:, :], sorted3[:, :, 1]))
            link(dve.memset(cont1[:, 0:1], 0.0))
            link(tt(cont1[:, 1:CH], sorted3[:, 1:CH, 2], sorted3[:, 0:CH - 1, 2], ALU.is_equal))
            link(dve.tensor_copy(cslast[:, 0:1], sorted3[:, 0, 2:3]))
            link(dve.tensor_copy(cslast[:, 1:2], sorted3[:, CH - 1, 2:3]))
            dve.tensor_copy(fixi[:, 2:3], cslast[:, 0:1]).then_inc(firstsrc_ready, 1)
            link(ts(tA, ident[:, :], cslast[:, 0:1], ALU.mult))
            dve.tensor_scalar(tB, ident[:, :], cslast[:, 1:2], None, ALU.mult).then_inc(diag1_ready, 1)
            dve.tensor_tensor(endf, base, cnt, ALU.add).then_inc(ends1_ready, 1)
            dve.wait_ge(ends1_ready, 1)
            dve.wait_ge(diag1_done, 1)
            chain_masks(1, cslast[:, 0:1], cslast[:, 1:2])
            link(ts(has, cnt, 0.0, ALU.is_gt))
            link(stt(scr, endf, float(-1 - EP), has, ALU.add, ALU.mult))
            link(ts(nidx[:, 2, 0:NB], scr, float(EP), ALU.add))
            dve.wait_ge(first1_end, 16)
            link(tt(chunkf[:, 1:2], fixr[:, 0:1], chunkf[:, 0:1], ALU.min))
            dve.tensor_scalar(fixi[:, 2:3], chunkf[:, 1:2], -1.0, None, ALU.add).then_inc(order_ready, 1)
            dve.wait_ge(order_ready, 1)

            dve.wait_ge(zeroed, 16 * NG)
            dve.wait_ge(attr_ready, 32)
            aq = Steps(n_act)
            ad = Steps(n_actd)
            x = Steps(n_x)
            mm = Steps(n_mm)
            ff2 = Steps(n_ff2)
            stg = Steps(n_stage, 1)
            usd = Steps(nrow_used, 1)
            f1 = t1[:, :, 0:D]
            f2 = t2[:, :, 0:D]
            f3 = msg[:, 0:KB * D].rearrange("p (b d) -> p b d", d=D)
            tn = Steps(n_t)
            kp = Steps(n_kept)

            def bcol(name):
                return bias[:, bb(name), :].unsqueeze(1).to_broadcast([P, KB, D])

            def h4(ap, h):
                return ap.rearrange("p b (h d) -> p b h d", h=h)

            def sm(k, h):
                return small[:, k, 0:KB * h].rearrange("p (b h) -> p b h", h=h)

            def ask(ins):
                ins.then_inc(n_act, 1)
                aq.add()
                ad.add()
                dve.wait_ge(n_actd, ad.value())

            def norm(t, tmp, h, o_, last=None):
                n = D // h
                full = [P, KB, h, n]
                link(red(sm(0, h), h4(t, h)))
                link(ts(sm(0, h), sm(0, h), 1.0 / n, ALU.mult))
                link(tt(h4(t, h), h4(t, h), sm(0, h).unsqueeze(3).to_broadcast(full), ALU.subtract))
                link(tt(h4(tmp, h), h4(t, h), h4(t, h), ALU.mult))
                ask(red(sm(1, h), h4(tmp, h)))
                link(dve.reciprocal(sm(1, h), sm(1, h)))
                m = tt(h4(o_, h), h4(t, h), sm(1, h).unsqueeze(3).to_broadcast(full), ALU.mult)
                if last is None:
                    link(m)
                else:
                    tell(m, last)

            nscat = 0
            for ph in range(6):
                if ph < 5:
                    st4 = stage[:, 0:KB * GW[ph]].rearrange("p (b w) -> p b w", b=KB)
                    if ph == 0:
                        link(dve.memset(st4[:, :, 256:257], 1.0))
                    elif ph == 2:
                        link(dve.memset(h4(st4[:, :, D:GW[2]], 8)[:, :, :, 16:17], 1.0))
                    else:
                        link(dve.memset(h4(st4[:, :, 0:132], 4)[:, :, :, 32:33], 1.0))
                if ph > 0:
                    R = nrow[:, 0:KB * SW[ph - 1]].rearrange("p (b w) -> p b w", b=KB)
                    H, d1, F = HEADS[ph - 1], HD1[ph - 1], FW[ph - 1]
                def features(g, first=False, between=None):
                    Xg = X[:, grp(g), :]
                    Ag = aux[:, grp(g), 0:D]
                    if not first and ph < 5:
                        dve.wait_ge(n_t, tn.value())
                    if ph in (1, 2, 3) and not first or ph in (2, 3, 4) and first:
                        dve.wait_ge(n_kept, kp.value())
                    kp.add(int(ph in (1, 2, 3)))
                    tn.add(XS[ph])
                    if ph == 0:
                        tell(cp(f1, Xg), x)
                    else:
                        dve.wait_ge(nrow_in, g * (16 * KB) + (16 * KB + (ph - 1) * 16 * NB))
                    if ph == 1:
                        link(tt(f1, Xg, R[:, :, D:D + 1].to_broadcast([P, KB, D]), ALU.mult))
                        tell(tt(f1, f1, R[:, :, 0:D], ALU.subtract), usd)
                        link(tt(f2, Ag, indeg[:, grp(g)].unsqueeze(2).to_broadcast([P, KB, D]), ALU.mult))
                        link(tt(f1, f1, f2, ALU.add))
                        link(tt(f1, f1, Xg, ALU.add))
                        norm(f1, f2, 1, f1, x)
                    if ph == 2:
                        Rh = h4(R[:, :, 0:F], 4)
                        link(ts(sm(2, 4), Rh[:, :, :, 32], 1e-10, ALU.max))
                        link(dve.reciprocal(sm(2, 4), sm(2, 4)))
                        tell(tt(h4(f1, 4), Rh[:, :, :, 0:32], sm(2, 4).unsqueeze(3).to_broadcast([P, KB, 4, 32]), ALU.mult), usd)
                        norm(f1, f2, 4, f1)
                        link(tt(f1, f1, bcol("scale0"), ALU.mult))
                        link(tt(f1, f1, bcol("offset0"), ALU.add))
                        link(tt(f1, f1, Ag, ALU.add))
                        link(stt(f1, f1, 0.5, Xg, ALU.mult, ALU.add))
                        norm(f1, f2, 1, f1, x)
                    if ph == 3:
                        Rh = h4(R[:, :, 0:F], 8)
                        link(ts(sm(2, 8), Rh[:, :, :, 16], 1e-8, ALU.add))
                        link(dve.reciprocal(sm(2, 8), sm(2, 8)))
                        tell(tt(h4(f1, 8), Rh[:, :, :, 0:16], sm(2, 8).unsqueeze(3).to_broadcast([P, KB, 8, 16]), ALU.mult), x)
                        tell(dve.memset(small[:, 11, 0:1], 0.0), usd)
                        if between:
                            between()
                        mm.add()
                        dve.wait_ge(n_mm, mm.value())
                        link(tt(f2, mmX, bcol("L2_gnn_bo"), ALU.add))
                        link(tt(f2, f2, Xg, ALU.add))
                        norm(f2, f1, 1, f2)
                        link(tt(f2, f2, bcol("L2_gnn_ln1_g"), ALU.mult))
                        tell(tt(f2, f2, bcol("L2_gnn_ln1_b"), ALU.add), x)
                        ff2.add()
                        dve.wait_ge(n_ff2, ff2.value())
                        link(tt(f1, mmX, bcol("L2_gnn_b2"), ALU.add))
                        link(tt(f1, f1, f2, ALU.add))
                        norm(f1, f2, 1, f1)
                        link(tt(f1, f1, bcol("L2_gnn_ln2_g"), ALU.mult))
                        link(tt(f1, f1, bcol("L2_gnn_ln2_b"), ALU.add))
                        link(tt(f1, f1, Xg, ALU.add))
                        norm(f1, f2, 1, f1, x)
                    if ph in (4, 5):
                        Rh = h4(R[:, :, 0:F], 4)
                        mR = R[:, :, F:F + 4]
                        own = aux[:, grp(g), D:D + 4]
                        e1 = small[:, 4, 0:28].rearrange("p (b h) -> p b h", h=4)
                        e2 = small[:, 4, 28:56].rearrange("p (b h) -> p b h", h=4)
                        link(tt(sm(5, 4), mR, own, ALU.max))
                        link(tt(small[:, 3, 0:28].rearrange("p (b h) -> p b h", h=4), mR, sm(5, 4), ALU.subtract))
                        ask(tt(small[:, 3, 28:56].rearrange("p (b h) -> p b h", h=4), own, sm(5, 4), ALU.subtract))
                        link(tt(sm(6, 4), Rh[:, :, :, 32], e1, ALU.mult))
                        link(tt(sm(6, 4), sm(6, 4), e2, ALU.add))
                        link(dve.reciprocal(sm(6, 4), sm(6, 4)))
                        tell(tt(h4(f1, 4), Rh[:, :, :, 0:32], e1.unsqueeze(3).to_broadcast([P, KB, 4, 32]), ALU.mult), usd)
                        link(tt(h4(f2, 4), h4(Ag, 4), e2.unsqueeze(3).to_broadcast([P, KB, 4, 32]), ALU.mult))
                        link(tt(f1, f1, f2, ALU.add))
                        link(tt(h4(f1, 4), h4(f1, 4), sm(6, 4).unsqueeze(3).to_broadcast([P, KB, 4, 32]), ALU.mult))
                        link(tt(f1, f1, bcol("L3_gnn_b1" if ph == 4 else "L3_gnn_b2"), ALU.add))
                        if ph == 4:
                            tell(ts(f1, f1, 0.0, ALU.max), x)
                        else:
                            link(ts(f1, f1, 0.0, ALU.max))
                            link(tt(f1, f1, Xg, ALU.add))
                            norm(f1, f2, 1, Xg, stg)

                def tables(g):
                    Ag = aux[:, grp(g), 0:D]
                    mm.add()
                    dve.wait_ge(n_mm, mm.value())
                    dve.wait_ge(tab_saved, g * 16 + (16 + 16 * KG * ph))
                    z3 = zst[:, 0:KB * ZW[ph]].rearrange("p (b w) -> p b w", b=KB)

                    def spread_free():
                        dve.wait_ge(dtab_saved, g * 16 + (16 + 16 * KG * nscat))
                        dve.wait_ge(group_over, g + (1 + KG * nscat))

                    m1 = mm256[:, :, 0:D]
                    m2 = mm256[:, :, D:2 * D]
                    if ph == 0:
                        link(cp(st4[:, :, 0:D], m1))
                        link(cp(st4[:, :, D:2 * D], X[:, grp(g), :]))
                        link(tt(Ag, m2, bcol("L0_gnn_b4"), ALU.add))
                        spread_free()
                        tell(tt(z3, m1, bcol("L0_gnn_b1"), ALU.add), stg)
                    if ph == 1:
                        sv = h4(st4[:, :, 0:132], 4)[:, :, :, 0:32]
                        link(tt(f2, m2, bcol("L1_gnn_b1"), ALU.add))
                        link(ts(sv, h4(f2, 4), 0.0, ALU.max))
                        link(tt(h4(f2, 4), sv, h4(bcol("att"), 4), ALU.mult))
                        link(red(sm(2, 4), h4(f2, 4)))
                        link(tt(f3, m1, bcol("L1_gnn_b0"), ALU.add))
                        tell(stt(st4[:, :, 132:136], sm(2, 4), 0.2, sm(2, 4), ALU.mult, ALU.max), stg)
                        link(ts(f3, f3, 0.0, ALU.max))
                        norm(f3, f2, 4, f3)
                        link(tt(f3, f3, bcol("scale1"), ALU.mult))
                        link(tt(Ag, f3, bcol("offset1"), ALU.add))
                    if ph == 2:
                        link(tt(st4[:, :, 0:D], m1, bcol("L2_gnn_bq"), ALU.add))
                        link(tt(h4(st4[:, :, D:GW[2]], 8)[:, :, :, 0:16], h4(mmX, 8), h4(bcol("L2_gnn_bv"), 8), ALU.add))
                        spread_free()
                        tell(tt(z3, m2, bcol("L2_gnn_bk"), ALU.add), stg)
                    if ph in (3, 4):
                        link(cp(h4(st4[:, :, 0:132], 4)[:, :, :, 0:32], h4(m1, 4)))
                        link(cp(Ag, m1))
                        link(cp(st4[:, :, 132:136], mm256[:, :, D:D + 4]))
                        spread_free()
                        link(cp(z3, mm256[:, :, D + 4:D + 8]))
                        link(tt(sm(2, 4), st4[:, :, 132:136], z3, ALU.add))
                        tell(stt(aux[:, grp(g), D:D + 4], sm(2, 4), 0.2, sm(2, 4), ALU.mult, ALU.max), stg)

                features(0, first=True)
                with dve.Fori(0, KG - 1) as it:
                    for q, per in ((st, KD[ph]), (aq, NAC[ph]), (ad, NAC[ph]), (x, XS[ph]), (mm, [1, 1, 1, 2, 1, 0][ph]),
                                   (ff2, int(ph == 3)), (stg, 1), (usd, int(ph > 0)), (tn, XS[ph]), (kp, int(ph in (1, 2, 3)))):
                        q.loop(it, per)
                    if ph == 3:
                        features(it + 1, between=lambda: tables(it))
                    else:
                        features(it + 1)
                        if ph < 5:
                            tables(it)
                for q in (st, aq, ad, x, mm, ff2, stg, usd, tn, kp):
                    q.close(KG - 1)
                if ph < 5:
                    tables(KG - 1)
                if ph == 5:
                    continue
                if ZW[ph]:
                    nscat += 1

                H, d1, F, W, V = HEADS[ph], HD1[ph], FW[ph], SW[ph], VO[ph]
                n = H * (B + 1)

                def hb(ap):
                    return ap[:, 0:n].rearrange("p (h b) -> p h b", h=H)

                if ZW[ph] == 4:
                    dve.wait_ge(slim_in, 16 * (ph - 2))
                    z = rows[:, 0:CH * 4].rearrange("p (c h) -> p c h", h=4)
                    for h in range(4):
                        m = dve.tensor_tensor_scan(ebuf[:, h * CH:(h + 1) * CH], cont[:, :], z[:, :, h], 0.0, ALU.mult, ALU.add)
                        if h < 3:
                            link(m)
                    m.then_inc(slim_done, 1)
                    dve.wait_ge(slim_done, ph - 2)
                e3 = ebuf[:, :].rearrange("p (h c) -> p h c", c=CH)
                for s in range(2):
                    dve.wait_ge(sums_saved[s], 16 + 16 * IT * ph)
                link(dve.memset(sums[:, (2 * B - 1) * W:2 * B * W], 0.0))
                link(dve.memset(dstf[:, 1, B - 1, :], 0.0)) if ZW[ph] == D else None
                link(dve.memset(mx[:, :], 0.0))
                kept = Steps(ebias_kept, 1)
                du = Steps(dst_used, 1 + NG * [0, 0, 1, 0, 0][ph])
                su = Steps(sums_ready, NG * ph)
                ru = Steps(rows_used, 2 + NG * ph)
                sr = Steps(scores_ready, NG * ph)
                holds = Steps(hold_step, (B - 1) * NG * [0, 0, 1, 0, 0][ph])
                accs = Steps(acc_step, (B - 1) * NG * ph)
                parts = Steps(msg_ready)
                wide = int(ZW[ph] == D)

                def expect(g, s, between=None):
                    copied = cp(cg[:, s, :], (cont1 if ph == 1 else cont)[:, bass.ds(g * B, B)])
                    if between:
                        note(copied)
                        between()
                    else:
                        link(copied)
                    if ph:
                        link(ts(hb(nf)[:, :, 1:B + 1], cg[:, s, :].unsqueeze(1).to_broadcast([P, H, B]), -1.0, ALU.add, BIG, ALU.mult))

                def hold(s, j):
                    prev = dstf[:, s, j - 1, :] if j else dstf[:, 1 - s, B - 1, :]
                    if j:
                        dve.wait_ge(hold_step, holds.value())
                    m = stt(dstf[:, s, j, :], prev, cg[:, s, j:j + 1], dstf[:, s, j, :], ALU.mult, ALU.add)
                    if j < B - 1:
                        m.then_inc(hold_step, 1)
                        holds.add()
                    else:
                        m.then_inc(dst_used, 1)
                        du.add()

                def turn(it, last):
                    for s in range(2):
                        g = it * 2 + s
                        ahead = not (last and s)
                        G3 = rows[:, s * B * GW[ph]:(s + 1) * B * GW[ph]].rearrange("p (b w) -> p b w", b=B)
                        S3 = sums[:, s * B * W:(s + 1) * B * W].rearrange("p (b w) -> p b w", b=B)
                        Sp = sums[:, ((2 - s) * B - 1) * W:(2 - s) * B * W]
                        ce = bass.ds(g * B, B)
                        if ph == 1:
                            dve.wait_ge(ebias_done, g + 2)
                            tell(tt(e3[:, :, ce], psX[:, 0:8 * B].rearrange("p (b h) -> p h b", h=8),
                                    beb[:, :].unsqueeze(2).to_broadcast([P, 8, B]), ALU.add), kept)
                        dve.wait_ge(rows_landed[s], it * (16 * B) + (16 * B + ph * IT * 16 * B))
                        if ph == 0:
                            G1 = G3[:, :, 0:D]
                            link(tt(G1, dstf[:, s, :, :], G1, ALU.subtract))
                            link(stt(G1, G1, 0.0, bias[:, bb("L0_gnn_W2"), :].unsqueeze(1).to_broadcast([P, B, D]), ALU.max, ALU.mult))
                            tell(red(ex[:, s * B:(s + 1) * B], G1), sr)
                            if ahead:
                                expect(g + 1, 1 - s)
                            dve.wait_ge(gate_ready, g + 1)
                            link(ts(wt[:, s, :], ex[:, s * B:(s + 1) * B], 1.0, ALU.add))
                            tell(dve.reciprocal(wt[:, s, :], wt[:, s, :]), wr)
                            dve.wait_ge(sums_saved[s], it * 16 + 16)
                        else:
                            note(cp(hb(sc)[:, :, 0], hb(mx)[:, :, B]))
                            s3 = hb(sc)[:, :, 1:B + 1]
                            if ph == 1:
                                link(cp(s3, G3[:, :, 132:136].rearrange("p b h -> p h b")))
                            if ph == 2:
                                link(tt(G3[:, :, 0:D], G3[:, :, 0:D], dstf[:, s, :, :], ALU.mult))
                                link(red(s3.rearrange("p h b -> p b h"), h4(G3[:, :, 0:D], 8)))
                                link(stt(s3, s3, 0.25, e3[:, :, ce], ALU.mult, ALU.add))
                            if ph >= 3:
                                link(tt(s3, G3[:, :, 132:136].rearrange("p b h -> p h b"), e3[:, 0:4, ce], ALU.add))
                                link(stt(s3, s3, 0.2, s3, ALU.mult, ALU.max))
                            link(dve.tensor_tensor_scan(fm[:, 0:n], nf[:, 0:n], sc[:, 0:n], 0.0, ALU.add, ALU.max))
                            link(dve.tensor_tensor_scan(mx[:, 0:n][:, ::-1], nf[:, 1:n + 1][:, ::-1], fm[:, 0:n][:, ::-1], 0.0, ALU.add, ALU.max))
                            tell(tt(df[:, 0:n], sc[:, 0:n], mx[:, 0:n], ALU.subtract), sr)

                            def keep_max():
                                dve.wait_ge(sums_saved[s], it * 16 + (16 + 16 * IT * ph))
                                link(cp(S3[:, :, F:F + H].rearrange("p b h -> p h b"), hb(mx)[:, :, 1:B + 1]))

                            if ahead:
                                expect(g + 1, 1 - s, between=keep_max)
                            else:
                                keep_max()
                            dve.wait_ge(weights_ready, g + (1 + NG * ph))
                            e3x = hb(ex)[:, :, 1:B + 1]
                            if ph == 1:
                                link(tt(e3x, e3x, ew[:, ce].unsqueeze(1).to_broadcast([P, H, B]), ALU.mult))
                            note(tt(fixr[:, 0:F].rearrange("p (h d) -> p h d", h=H), Sp[:, 0:F].rearrange("p (h d) -> p h d", h=H),
                                    hb(ex)[:, :, 0].unsqueeze(2).to_broadcast([P, H, d1]), ALU.mult))
                            tell(tt(msg[:, 0:B * F].rearrange("p (b h d) -> p b h d", b=B, h=H), h4(G3[:, :, V:V + F], H),
                                    e3x.rearrange("p h b -> p b h").unsqueeze(3).to_broadcast([P, B, H, d1]), ALU.mult), ru)
                            dve.wait_ge(dve_step, st.value())
                        if wide and ahead:
                            nxt = (it + s) * 16 + (16 + 16 * IT * [0, 0, 1][ph])
                            dve.wait_ge(dst_landed[1 - s], nxt)
                        for j in range(B):
                            if ph == 0 and j in [0] + [k + 1 for k in MSG_PARTS[:-1]]:
                                if j <= MSG_PARTS[-2]:
                                    parts.add()
                                    dve.wait_ge(msg_ready, parts.value())
                                else:
                                    dve.wait_ge(rows_used, g + 3)
                            if j:
                                dve.wait_ge(acc_step, accs.value())
                                prev = S3[:, j - 1, 0:F]
                            else:
                                prev = fixr[:, 0:F] if ph else Sp[:, 0:F]
                            m = stt(S3[:, j, 0:F], prev, cg[:, s, j:j + 1], msg[:, j * F:(j + 1) * F], ALU.mult, ALU.add)
                            if j < B - 1:
                                m.then_inc(acc_step, 1)
                                accs.add()
                            else:
                                m.then_inc(sums_ready, 1)
                                su.add()
                            if wide and ahead:
                                hold(1 - s, j)
                        dve.wait_ge(sums_ready, su.value())
                        if wide and ahead:
                            dve.wait_ge(dst_used, du.value())

                wr = Steps(weights_ready)
                expect(0, 0)
                if wide:
                    dve.wait_ge(dst_landed[0], 16 + 16 * IT * [0, 0, 1][ph])
                    for j in range(B):
                        hold(0, j)
                    dve.wait_ge(dst_used, du.value())
                counts = ((st, KE[ph]), (kept, 2 * int(ph == 1)), (du, 2 * wide), (su, 2), (ru, 2 * int(ph > 0)), (sr, 2),
                          (wr, 2 * int(ph == 0)), (holds, 2 * (B - 1) * wide), (accs, 2 * (B - 1)), (parts, 6 * int(ph == 0)))
                with dve.Fori(0, IT - 1) as it:
                    for q, per in counts:
                        q.loop(it, per)
                    turn(it, False)
                for q, _ in counts:
                    q.close(IT - 1)
                turn(IT - 1, True)

                last = sums[:, (2 * B - 1) * W:2 * B * W]
                if ph == 0:
                    dve.wait_ge(st_carry, 1)
                    dve.wait_ge(fix_in, 16)
                    dve.tensor_tensor(fixr[:, 0:F], fixr[:, 0:F], psX[:, 0:F], ALU.add).then_inc(fix_ready, 1)
                    dve.wait_ge(fix_ready, 1)
                    continue
                three = [P, H, P]
                dg = dflat[:, 0:H * P].rearrange("p (h c) -> p h c", h=H)
                vv = dflat[:, 1024:1024 + H * P].rearrange("p (h c) -> p h c", h=H)
                dve.tensor_tensor(dg, ident[:, :].unsqueeze(1).to_broadcast(three), last[:, F:F + H].unsqueeze(2).to_broadcast(three),
                                  ALU.mult).then_inc(st_diag, 1)
                dve.wait_ge(st_max, ph)
                link(tt(vv, psMf[:, 0:H * P].rearrange("p (h c) -> p h c", h=H), fars[int(ph == 1)][:, :].unsqueeze(1).to_broadcast(three), ALU.add))
                link(red(fixk[:, 0:H], vv, ALU.max))
                dve.tensor_tensor(vv, vv, fixk[:, 0:H].unsqueeze(2).to_broadcast(three), ALU.subtract).then_inc(st_diff, 1)
                dve.wait_ge(fix_in, 16 * (ph + 1))
                link(tt(fixk[:, 8:8 + H], fixk[:, 0:H], fixr[:, F:F + H], ALU.max))
                link(tt(fixm[:, 0, 0:H], fixr[:, F:F + H], fixk[:, 8:8 + H], ALU.subtract))
                dve.tensor_tensor(fixm[:, 1, 0:H], fixk[:, 0:H], fixk[:, 8:8 + H], ALU.subtract).then_inc(fix_pair, 1)
                dve.wait_ge(fix_exp, ph)
                dve.wait_ge(st_carry, ph + 1)

                def hd(ap):
                    return ap.rearrange("p (h d) -> p h d", h=H)

                link(tt(hd(msg[:, 0:F]), hd(psX[:, 0:F]), fixm[:, 3, 0:H].unsqueeze(2).to_broadcast([P, H, d1]), ALU.mult))
                link(tt(hd(fixr[:, 0:F]), hd(fixr[:, 0:F]), fixm[:, 2, 0:H].unsqueeze(2).to_broadcast([P, H, d1]), ALU.mult))
                link(tt(fixr[:, 0:F], fixr[:, 0:F], msg[:, 0:F], ALU.add))
                dve.tensor_copy(fixr[:, F:F + H], fixk[:, 8:8 + H]).then_inc(fix_ready, 1)
                dve.wait_ge(fix_ready, ph + 1)


_IN = ["x", "src", "dst", "edge_attr_32", "edge_weight", "L0_gnn_W1", "L0_gnn_b1", "L0_gnn_W2", "L0_gnn_b2",
       "L0_gnn_W4", "L0_gnn_b4", "L1_gnn_W0", "L1_gnn_b0", "L1_gnn_W1", "L1_gnn_b1", "L2_gnn_Wq", "L2_gnn_bq",
       "L2_gnn_Wk", "L2_gnn_bk", "L2_gnn_Wv", "L2_gnn_bv", "L2_gnn_We", "L2_gnn_be", "L2_gnn_Wo", "L2_gnn_bo",
       "L2_gnn_ln1_g", "L2_gnn_ln1_b", "L2_gnn_W1", "L2_gnn_b1", "L2_gnn_W2", "L2_gnn_b2", "L2_gnn_ln2_g",
       "L2_gnn_ln2_b", "L3_gnn_W1", "L3_gnn_a_src1", "L3_gnn_a_dst1", "L3_gnn_b1", "L3_gnn_W2", "L3_gnn_a_src2",
       "L3_gnn_a_dst2", "L3_gnn_b2"]


def kernel(**inputs):
    import numpy as _np
    import concourse.bacc as _bacc
    from concourse import mybir as _mybir
    from concourse.bass_utils import run_bass_kernel_spmd as _run

    named = {n: _np.asarray(inputs[n]) for n in _IN}
    for n in ("L1_gnn_W0", "L1_gnn_W1"):
        named[n] = named[n].T
    for n in ("L0_gnn_W2", "L3_gnn_a_src1", "L3_gnn_a_dst1", "L3_gnn_a_src2", "L3_gnn_a_dst2"):
        named[n] = named[n].reshape(-1)
    named["L2_gnn_b1"] = named["L2_gnn_b1"].reshape(4, 128).T
    attention, scale, offset = (_np.asarray(inputs["L1_gnn_" + n]) for n in ("attention", "scale", "offset"))
    named["att"] = attention[1].reshape(-1)
    for k in range(2):
        named[f"scale{k}"] = scale[k].reshape(-1)
        named[f"offset{k}"] = offset[k].reshape(-1)

    nc = _bacc.Bacc("TRN2", target_bir_lowering=False, num_devices=1)
    arrays, args = {}, {}
    for n, v in named.items():
        v = _np.ascontiguousarray(v)
        arrays[f"in_{n}"] = v
        args[n] = nc.dram_tensor(f"in_{n}", v.shape, _mybir.dt.from_np(v.dtype), kind="ExternalInput").ap()
    out = nc.dram_tensor("out_x", (6250, 128), _mybir.dt.float32, kind="ExternalOutput").ap()
    build(nc, args, out)
    return _run(nc, [arrays], core_ids=[0]).results[0]["out_x"]
```
